# Optimizing a Trainium2 kernel written in Bass

```python
import numpy as np
import jax
import jax.numpy as jnp

def _softmax(x, axis=-1):
    return jax.nn.softmax(x, axis=axis)

def _gelu(x):
    return jax.nn.gelu(x, approximate=True)

def _silu(x):
    return jax.nn.silu(x)

def _sigmoid(x):
    return jax.nn.sigmoid(x)

def _layernorm(x, axis=-1, eps=1e-05):
    m = jnp.mean(x, axis=axis, keepdims=True)
    v = jnp.var(x, axis=axis, keepdims=True)
    return (x - m) / jnp.sqrt(v + eps)

def _scatter_add(tgt, idx, src, axis=0):
    return tgt.at[idx].add(src)

def _segment_sum(src, seg, n):
    return jax.ops.segment_sum(src, seg, n)
kernel_name = 'mk_adj_resnorm_d2_adj_r2_d921f2'

def setup_inputs(seed: int=0):
    np.random.seed(seed)
    _w = jnp.asarray

    def _rec_inputs():
        import jax
        import jax.numpy as jnp
        _gk = jax.random.key(seed)
        x = -0.000125 + 0.9999 * jax.random.normal(jax.random.fold_in(_gk, 1), (16, 512, 128), jnp.float32)
        _a = jax.random.bernoulli(jax.random.fold_in(_gk, 2), 0.03125, (512, 512))
        _a = jnp.logical_or(_a, jnp.swapaxes(_a, -1, -2))
        _a = jnp.logical_or(_a, jnp.eye(512, dtype=bool))
        _af = _a.astype(jnp.float32)
        _af = _af * jax.random.uniform(jax.random.fold_in(_gk, 3), (512, 512), jnp.float32, 0.05, 0.000488281)
        adj = _af
        return (x, adj)
    x, adj = _rec_inputs()

    def _L0_gnn_setup():
        import jax, jax.numpy as jnp
        import numpy as np
        B, T, D, H = (64, 1024, 128, 128)
        MAX_SKIP = 4

        def _lstm_last(Wih, Whh, bih, bhh, xs):
            N, _, Hd = xs.shape
            bias = bih + bhh

            def step(carry, x_t):
                h, c = carry
                g = x_t @ Wih.T + h @ Whh.T + bias
                i, f, gg, o = jnp.split(g, 4, axis=-1)
                c = jax.nn.sigmoid(f) * c + jax.nn.sigmoid(i) * jnp.tanh(gg)
                h = jax.nn.sigmoid(o) * jnp.tanh(c)
                return ((h, c), None)
            init = (jnp.zeros((N, Hd), xs.dtype), jnp.zeros((N, Hd), xs.dtype))
            (h_last, _), _ = jax.lax.scan(step, init, jnp.swapaxes(xs, 0, 1))
            return h_last
        key = jax.random.key(seed)
        ks = jax.random.split(key, 8)
        s = 0.05
        x = jax.random.normal(ks[0], (B, T, D), jnp.float32)
        adj = jax.random.uniform(ks[1], (T, T), jnp.float32) / T
        Wg0 = jax.random.normal(ks[2], (D, H), jnp.float32) * s
        bg0 = jnp.zeros((H,), jnp.float32)
        Wg1 = jax.random.normal(ks[3], (H, H), jnp.float32) * s
        bg1 = jnp.zeros((H,), jnp.float32)
        Wih = jax.random.normal(ks[4], (MAX_SKIP, 4 * H, H), jnp.float32) * s
        Whh = jax.random.normal(ks[5], (MAX_SKIP, 4 * H, H), jnp.float32) * s
        bih = jax.random.normal(ks[6], (MAX_SKIP, 4 * H), jnp.float32) * s
        bhh = jax.random.normal(ks[7], (MAX_SKIP, 4 * H), jnp.float32) * s
        return dict(x=x, adj=adj, Wg0=Wg0, bg0=bg0, Wg1=Wg1, bg1=bg1, Wih=Wih, Whh=Whh, bih=bih, bhh=bhh)
    _L0_gnn_all = _L0_gnn_setup()
    _L0_gnn_in = {k: v for k, v in _L0_gnn_all.items() if k in ('Wg0', 'bg0', 'Wg1', 'bg1', 'Wih', 'Whh', 'bih', 'bhh')}
    del _L0_gnn_all

    def _L1_gnn_setup():
        import jax, jax.numpy as jnp
        import numpy as np
        BT, N, D, HEADS, E = (512, 64, 128, 4, 256)
        LRELU_SLOPE = 0.2
        EPS = 1e-08
        key = jax.random.key(seed)
        ks = jax.random.split(key, 8)
        d = D
        return {'H': jax.random.normal(ks[0], (BT, N, d), jnp.float32), 'W_lin': jax.random.normal(ks[1], (d, d), jnp.float32) / np.sqrt(d).astype(np.float32), 'W_val': jax.random.normal(ks[2], (d, d), jnp.float32) / np.sqrt(d).astype(np.float32), 'a': jax.random.normal(ks[3], (HEADS, d // HEADS), jnp.float32), 'W_out': jax.random.normal(ks[4], (d, d), jnp.float32) / np.sqrt(d).astype(np.float32), 'A0': jax.random.uniform(ks[5], (N, N), jnp.float32), 'src': jax.random.randint(ks[6], (E,), 0, N, jnp.int32), 'dst': jax.random.randint(ks[7], (E,), 0, N, jnp.int32)}
    _L1_gnn_all = _L1_gnn_setup()
    _L1_gnn_in = {k: v for k, v in _L1_gnn_all.items() if k in ('W_lin', 'W_val', 'a', 'W_out', 'src', 'dst')}
    del _L1_gnn_all
    return {'x': x, 'adj': adj, 'L0_gnn_Wg0': _L0_gnn_in['Wg0'], 'L0_gnn_bg0': _L0_gnn_in['bg0'], 'L0_gnn_Wg1': _L0_gnn_in['Wg1'], 'L0_gnn_bg1': _L0_gnn_in['bg1'], 'L0_gnn_Wih': _L0_gnn_in['Wih'], 'L0_gnn_Whh': _L0_gnn_in['Whh'], 'L0_gnn_bih': _L0_gnn_in['bih'], 'L0_gnn_bhh': _L0_gnn_in['bhh'], 'L1_gnn_W_lin': _L1_gnn_in['W_lin'], 'L1_gnn_W_val': _L1_gnn_in['W_val'], 'L1_gnn_a': _L1_gnn_in['a'], 'L1_gnn_W_out': _L1_gnn_in['W_out'], 'L1_gnn_src': _L1_gnn_in['src'], 'L1_gnn_dst': _L1_gnn_in['dst']}

def reference(x, adj, L0_gnn_Wg0, L0_gnn_bg0, L0_gnn_Wg1, L0_gnn_bg1, L0_gnn_Wih, L0_gnn_Whh, L0_gnn_bih, L0_gnn_bhh, L1_gnn_W_lin, L1_gnn_W_val, L1_gnn_a, L1_gnn_W_out, L1_gnn_src, L1_gnn_dst):
    import jax
    import jax.numpy as jnp

    def _L0_gnn_ref(x, adj, Wg0, bg0, Wg1, bg1, Wih, Whh, bih, bhh):
        import jax, jax.numpy as jnp
        import numpy as np
        B, T, D, H = (64, 1024, 128, 128)
        MAX_SKIP = 4

        def _lstm_last(Wih, Whh, bih, bhh, xs):
            N, _, Hd = xs.shape
            bias = bih + bhh

            def step(carry, x_t):
                h, c = carry
                g = x_t @ Wih.T + h @ Whh.T + bias
                i, f, gg, o = jnp.split(g, 4, axis=-1)
                c = jax.nn.sigmoid(f) * c + jax.nn.sigmoid(i) * jnp.tanh(gg)
                h = jax.nn.sigmoid(o) * jnp.tanh(c)
                return ((h, c), None)
            init = (jnp.zeros((N, Hd), xs.dtype), jnp.zeros((N, Hd), xs.dtype))
            (h_last, _), _ = jax.lax.scan(step, init, jnp.swapaxes(xs, 0, 1))
            return h_last
        h = jax.nn.relu(jnp.einsum('ts,bsh->bth', adj, x @ Wg0 + bg0))
        h = jax.nn.relu(jnp.einsum('ts,bsh->bth', adj, h @ Wg1 + bg1))
        Bv, Tv, Hd = h.shape
        for p in range(1, MAX_SKIP + 1):
            nw = Tv // p
            wins = h[:, :nw * p, :].reshape(Bv * nw, p, Hd)
            last = _lstm_last(Wih[p - 1], Whh[p - 1], bih[p - 1], bhh[p - 1], wins)
            idx = jnp.arange(nw) * p + (p - 1)
            h = h.at[:, idx, :].set(last.reshape(Bv, nw, Hd))
        return h

    def _L1_gnn_ref(H, W_lin, W_val, a, W_out, A0, src, dst):
        import jax, jax.numpy as jnp
        import numpy as np
        BT, N, D, HEADS, E = (512, 64, 128, 4, 256)
        LRELU_SLOPE = 0.2
        EPS = 1e-08
        bt, n, d = H.shape
        h, dh = a.shape
        Xq = (H @ W_lin.T).reshape(bt, n, h, dh)
        Xv = (H @ W_val.T).reshape(bt, n, h, dh)
        Qs = Xq[:, src]
        Kt = Xq[:, dst]
        e = jnp.einsum('behd,hd->beh', jax.nn.leaky_relu(Qs + Kt, LRELU_SLOPE), a)
        e = e + jnp.log(A0[src, dst] + EPS)[None, :, None]
        e_t = e.transpose(1, 0, 2)
        m = jax.ops.segment_max(e_t, src, num_segments=n)
        ex = jnp.exp(e_t - m[src])
        denom = jax.ops.segment_sum(ex, src, num_segments=n)
        attn = ex / denom[src]
        Vt = Xv[:, dst].transpose(1, 0, 2, 3)
        Y = jax.ops.segment_sum(attn[..., None] * Vt, src, num_segments=n)
        Y = Y.transpose(1, 0, 2, 3).reshape(bt, n, d)
        return Y @ W_out.T
    x = _layernorm(x + _L0_gnn_ref(x, adj, L0_gnn_Wg0, L0_gnn_bg0, L0_gnn_Wg1, L0_gnn_bg1, L0_gnn_Wih, L0_gnn_Whh, L0_gnn_bih, L0_gnn_bhh), axis=-1)
    x = _layernorm(x + _L1_gnn_ref(x, L1_gnn_W_lin, L1_gnn_W_val, L1_gnn_a, L1_gnn_W_out, adj, L1_gnn_src, L1_gnn_dst), axis=-1)
    return x

_drawn_inputs = setup_inputs


def setup_inputs(seed=0):
    import zlib

    import numpy as np

    out = dict(_drawn_inputs(seed))
    spreads = {'L0_gnn_bg0': (0.0, 0.8), 'L0_gnn_bg1': (0.0, 0.8)}
    factors = {'L0_gnn_Wg0': 8.0,
     'L0_gnn_Wg1': 7.45,
     'L0_gnn_Wih': 4.128,
     'L0_gnn_Whh': 8.0,
     'L0_gnn_bih': 2.731,
     'L0_gnn_bhh': 2.743}
    for name, (base, spread) in spreads.items():
        noise = np.random.default_rng([zlib.crc32(name.encode()), seed]).standard_normal(out[name].shape)
        drawn = base * np.exp(spread * noise) if base else spread * noise
        out[name] = jnp.asarray(drawn.astype(out[name].dtype))
    for name, factor in factors.items():
        out[name] = (out[name] * factor).astype(out[name].dtype)
    return out
```

```python
import concourse.bass as bass
from concourse import mybir
from contextlib import ExitStack

B, T, D = 16, 512, 128
G = 4
ITERS = B // G
NC = T // 128
HEADS, E = 4, 256
EC = E // 128
SKIPS = 4
R, Q = 12, 43
RFULL = T - R * (Q - 1)
CUT = RFULL * Q
W = 2 * G * Q
W4 = 3 * (G // 2) * Q
EPS = 1e-5
LOG_EPS = 1e-8
SLOPE = 0.2
FAR = 3e38
GI, GF, GG, GO = range(4)

C_ID, C_MASK, C_NODE, C_NROW, C_IOTA, C_EDGE, C_ONES, C_EALL, C_END = (
    0, 128, 192, 196, 708, 964, 966, 1094, 1606)


def lstm_jobs():
    jobs = [(1, 0, s, s % 3) for s in range(6)]
    for p, chunks in ((2, 3), (3, 2), (4, 2)):
        jobs += [(p, t, k, k) for t in range(p) for k in range(chunks)]
    return jobs


LSTM = lstm_jobs()
NL = len(LSTM)


def width(job):
    return W4 if job[0] == 4 else W


def gates_of(job):
    return [GI, GG, GO] if job[1] == 0 else [GI, GG, GF, GO]


def done_before(n):
    p, t, k, _ = LSTM[n]
    if p == 1:
        return 0
    last = {2: (1, 0, 2 * k + 1), 3: (2, 1, k + 1), 4: (3, 2, 1)}[p]
    return 1 + next(m for m, j in enumerate(LSTM) if j[:3] == last)


def last_user(n):
    return next((m for m in range(n - 1, -1, -1) if LSTM[m][3] == LSTM[n][3]), None)


GNN = ["U", "Z", "Z2", "H2"]
ATT = ["N", "GX", "QV", "SC", "AB0", "AB1", "MW", "OUT"]
JOBS = GNN + list(range(NL)) + ATT
assert len(JOBS) % 2 == 0
GATES = sum(len(gates_of(j)) for j in LSTM)


def gates_before(n):
    return sum(len(gates_of(j)) for j in LSTM[:n])


READ_OUT = {"U": ("u_ready", 4, 4), "Z": ("h1_ready", 4, 4), "Z2": ("z2_ready", 4, 4),
            "H2": ("h2_ready", 8, 8), "N": ("n_summed", 1, 1), "GX": ("gx_ready", 4, 4),
            "QV": ("v_copied", 2, 2), "SC": ("shifted", 1, 1), "AB0": ("m_ready", 2, 1),
            "AB1": ("m_ready", 2, 2), "MW": ("mw_ready", 2, 2)}
READ_OUT.update({n: ("gate_act", GATES, gates_before(n + 1)) for n in range(NL)})

DVE_LINKS = 75



def build(nc, x, adjT, consts, edge_col, edge_row, w_gnn, b_gnn0, b_gnn1, w_ih, w_hh, b_ih, b_hh,
          a_col, out):
    f32, f32r, i32 = mybir.dt.float32, mybir.dt.float32r, mybir.dt.int32
    ALU, ACT, AX = mybir.AluOpType, mybir.ActivationFunctionType, mybir.AxisListType
    HI, LO = 0, 1

    ctx = ExitStack()
    with ctx:
        def sb(name, shape, dt=f32):
            return ctx.enter_context(nc.sbuf_tensor(name, shape, dt))

        def sem(name):
            return ctx.enter_context(nc.semaphore(name))

        adj_s = sb("adj_s", [128, 2, NC, T], f32r)
        wg_s = sb("wg_s", [128, 2, 2, D], f32r)
        wa_s = sb("wa_s", [128, 2, 3, D], f32r)
        wl_s = sb("wl_s", [128, 2, 2, SKIPS, 4 * D], f32r)
        sel_g = sb("sel_g", [128, NC, 2 * E], f32r)
        sel_s = sb("sel_s", [128, EC, T], f32r)
        br_t = sb("br_t", [128, T])
        b1_t = sb("b1_t", [128, D])
        lbias = sb("lbias", [128, 2, SKIPS, 4])
        ident = sb("ident", [128, 128])
        eall = sb("eall", [16, G, 128])
        a_blk = sb("a_blk", [128, G, 16])
        log_b = sb("log_b", [16, E])
        seg = sb("seg", [16, 4, E])
        half_c = sb("half_c", [128, 1])
        eps8 = sb("eps8", [128, 1])

        x_in = sb("x_in", [128, 2, NC, D])
        buf_a = sb("buf_a", [128, 2, G, T], f32r)
        buf_b = sb("buf_b", [128, 2, G, T], f32r)
        h_t = sb("h_t", [128, 2, R, G, Q], f32r)
        gates = sb("gates", [128, 3, 4, W])
        cell = sb("cell", [128, 3, W])
        rec = sb("rec", [128, 3, 2, W], f32r)
        hn = sb("hn", [128, G, T])
        res = sb("res", [128, G, NC, D])
        buf_c = sb("buf_c", [128, 2, G, T], f32r)
        buf_d = sb("buf_d", [128, 2, G, T], f32r)
        stats = sb("stats", [128, G * NC, 6])
        mv = sb("mv", [128, G * NC, 2])
        rstd = sb("rstd", [128, G * NC])
        sm = sb("sm", [16, 3, E])

        ps = ctx.enter_context(nc.psum_tensor("ps", [128, 8, 512], f32))

        names = ("ld_x0 ld_x1 ld_res ld_adj ld_const ld_edge ld_w ld_lw ld_b st_out "
                 "setup_dve setup_pe setup_act setup_pool start "
                 "x_hi x_ready u_full u_hi u_ready z_full z_sum z_hi h1_ready z2_full z2_sum z2_hi z2_ready "
                 "h2_full h2_hi h2_ready gate_full gate_act cell_ready tanh_done h_ready "
                 "hn_ready n_full var_ready rstd_ready x1_norm x1_hi x1_ready gx_full gx_hi gx_ready "
                 "qv_full q_copied v_copied lrelu_ready sc_full shifted exp_done attn_ready ab_full "
                 "m_ready m_hi m_split mw_full mw_hi mw_ready out_full out_ready "
                 "n_summed out_summed ones_r dve_chain").split()
        S = {n: sem(n) for n in names}

        block = ctx.enter_context(nc.Block())

        def bank(job, n):
            return ps[:, 4 * (JOBS.index(job) % 2) + n, :]

        def toks(hl, job, step=None):
            p, t, k, _ = job
            t = t if step is None else step
            if p == 1:
                return h_t[:, hl, 2 * k:2 * k + 2, :, :].rearrange("p r b q -> p r (b q)")
            if p == 2:
                return h_t[:, hl, 4 * k + t:4 * k + t + 3:2, :, :].rearrange("p r b q -> p r (b q)")
            if p == 3:
                return h_t[:, hl, 6 * k + t:6 * k + t + 4:3, :, :].rearrange("p r b q -> p r (b q)")
            h = G // 2
            return h_t[:, hl, t:t + 9:4, h * k:h * k + h, :].rearrange("p r b q -> p r (b q)")

        def cols(ap, job):
            n = 3 if job[0] == 4 else 2
            return ap[:, 0:width(job)].rearrange("p (r c) -> p r c", r=n)

        def pieces(b):
            for r0, r1, c0, c1, q in ((0, RFULL, 0, CUT, Q), (RFULL, R, CUT, T, Q - 1)):
                yield r0, r1, slice(c0, c1), q

        sc = hn[:, :, :].rearrange("p b t -> p (b t)")
        w_raw = sc[:, 0:5 * D]
        cst = gates[:, :, :, :].rearrange("p a b c -> p (a b c)")
        raw_adj = res[:, :, :, :].rearrange("p c t d -> p c (t d)")
        tmp = sc[:, 1024:2048]
        lw_raw = cst[:, 0:4096].rearrange("p (a s n) -> p a s n", a=2, s=SKIPS)

        const_t = cell[:, :, :].rearrange("p s c -> p (s c)")[:, 0:C_EALL - C_NODE]
        def C(a, b):
            return const_t[:, a - C_NODE:b - C_NODE]
        edge_i = sb("edge_i", [128, 4], i32)
        edgerow_i = x_in[0:1, 0, :, :].rearrange("p c d -> p (c d)").bitcast(i32)
        edge_f = sb("edge_f", [128, 4])
        small = sb("small", [128, 24])
        ones_r = rec[:, 0, HI, 0:128]

        @block.sync
        def _(sp):
            sp.dma_start(raw_adj, adjT).then_inc(S["ld_adj"], 16)
            sp.dma_start(w_raw, w_gnn).then_inc(S["ld_w"], 16)
            sp.dma_start(lw_raw[:, 0, :, :], w_ih).then_inc(S["ld_lw"], 16)
            sp.dma_start(lw_raw[:, 1, :, :], w_hh).then_inc(S["ld_lw"], 16)
            for it in range(ITERS):
                for b in range(G):
                    if G * it + b >= 2:
                        sp.wait_ge(S["x_ready"], G * it + b - 1)
                    elif b == 0:
                        sp.wait_ge(S["setup_dve"], 1)
                    sp.dma_start(x_in[:, b % 2, :, :], x[it, :, b]).then_inc(S[f"ld_x{b % 2}"], 16)
                if it == 0:
                    sp.wait_ge(S["start"], 1)
                else:
                    sp.wait_ge(S["out_ready"], it)
                    sp.dma_start(out[it - 1], res[:, :, :, :]).then_inc(S["st_out"], 16)
                    sp.wait_ge(S["st_out"], 16 * it)
                sp.dma_start(res[:, :, :, :], x[it]).then_inc(S["ld_res"], 16)
            sp.wait_ge(S["out_ready"], ITERS)
            sp.dma_start(out[ITERS - 1], res[:, :, :, :]).then_inc(S["st_out"], 16)
            sp.wait_ge(S["st_out"], 16 * ITERS)

        @block.gpsimd
        def _(pool):
            pool.memset(half_c[:, :], -0.5).then_inc(S["setup_pool"], 1)
            pool.memset(eps8[:, :], LOG_EPS).then_inc(S["setup_pool"], 1)
            pool.memset(ones_r.bitcast(f32), 1.0).then_inc(S["ones_r"], 1)
            pool.memset(seg[:, :, :], 0.0).then_inc(S["setup_pool"], 1)
            pool.memset(h_t[:, :, :, :, :].bitcast(f32), 0.0).then_inc(S["setup_pool"], 1)

            def inverse_deviation(k):
                pool.wait_ge(S["var_ready"], 2 * i + k + 1)
                pool.tensor_tensor(rstd[:, :], rstd[:, :], half_c[:, 0:1].broadcast_to([128, G * NC]),
                                   ALU.pow).then_inc(S["rstd_ready"], 1)

            with pool.Fori(0, ITERS) as i:
                inverse_deviation(0)
                for b in range(G):
                    pool.wait_ge(S["x1_hi"], 4 * i + b + 1)
                    pool.tensor_tensor(buf_c[:, LO, b, :], res[:, b, :, :].rearrange("p c d -> p (c d)"),
                                       buf_c[:, HI, b, :].bitcast(f32), ALU.subtract).then_inc(S["x1_ready"], 1)
                inverse_deviation(1)

        @block.scalar
        def _(act):
            act.dma_start(const_t, consts[:, C_NODE:C_EALL]).then_inc(S["ld_const"], 16)
            act.dma_start(ident[:, :], consts[:, C_ID:C_ID + 128]).then_inc(S["ld_const"], 16)
            act.dma_start(a_blk[:, :, :].rearrange("p b h -> p (b h)"),
                          consts[:, C_MASK:C_MASK + 64]).then_inc(S["ld_const"], 16)
            act.dma_start(eall[:, :, :].rearrange("p b h -> p (b h)"),
                          consts[0:16, C_EALL:C_EALL + 512]).then_inc(S["ld_const"], 16)
            act.dma_start(edge_i[:, :], edge_col).then_inc(S["ld_edge"], 16)
            act.dma_start(edgerow_i[:, 0:2 * E], edge_row).then_inc(S["ld_edge"], 16)
            act.dma_start(small[:, 0:1], b_gnn0).then_inc(S["ld_b"], 16)
            act.dma_start(small[:, 1:2], a_col).then_inc(S["ld_b"], 16)
            act.dma_start(lbias[:, 0, :, :], b_ih).then_inc(S["ld_b"], 16)
            act.dma_start(lbias[:, 1, :, :], b_hh).then_inc(S["ld_b"], 16)
            act.dma_start(b1_t[0:1, :], b_gnn1).then_inc(S["ld_b"], 16)
            act.wait_ge(S["ld_adj"], 16)
            act.activation(adj_s[:, HI, :, :], raw_adj, ACT.Copy).then_inc(S["setup_act"], 1)
            act.wait_ge(S["ld_w"], 16)
            act.activation(wg_s[:, HI, :, :].rearrange("p a n -> p (a n)"), w_raw[:, 0:2 * D], ACT.Copy).then_inc(S["setup_act"], 1)
            act.activation(wa_s[:, HI, :, :].rearrange("p a n -> p (a n)"), w_raw[:, 2 * D:5 * D], ACT.Copy).then_inc(S["setup_act"], 1)
            act.wait_ge(S["ld_lw"], 32)
            for m in range(2):
                act.activation(wl_s[:, HI, m, :, :], lw_raw[:, m, :, :], ACT.Copy).then_inc(S["setup_act"], 1)
            act.wait_ge(S["setup_pool"], 2)
            act.wait_ge(S["setup_pe"], 6)
            act.activation(log_b[:, :], ps[0:16, 6, 0:E], ACT.Ln, bias=eps8[0:16, :]).then_inc(S["setup_act"], 1)

            with act.Fori(0, ITERS) as i:
                for b in range(G):
                    act.wait_ge(S[f"ld_x{b % 2}"], 32 * i + 16 * (b // 2) + 16)
                    if b == 0:
                        act.wait_ge(S["z2_full"], 4 * i + 1)
                    act.activation(buf_a[:, HI, b, :], x_in[:, b % 2, :, :].rearrange("p c d -> p (c d)"),
                                   ACT.Copy).then_inc(S["x_hi"], 1)
                for b in range(G):
                    act.wait_ge(S["u_full"], 4 * i + b + 1)
                    act.activation(buf_b[:, HI, b, :], bank("U", b), ACT.Copy).then_inc(S["u_hi"], 1)
                for b in range(G):
                    act.wait_ge(S["z_sum"], 4 * i + b + 1)
                    act.activation(buf_a[:, HI, b, :], bank("Z", b), ACT.Relu).then_inc(S["z_hi"], 1)
                for b in range(G):
                    act.wait_ge(S["z2_sum"], 4 * i + b + 1)
                    act.activation(buf_b[:, HI, b, :], bank("Z2", b), ACT.Copy).then_inc(S["z2_hi"], 1)
                act.wait_ge(S["hn_ready"], 2 * i + 1)
                for b in range(G):
                    act.wait_ge(S["h2_full"], 4 * i + b + 1)
                    for r0, r1, c, q in pieces(b):
                        act.activation(h_t[:, HI, r0:r1, b, 0:q],
                                       bank("H2", b)[:, c].rearrange("p (r q) -> p r q", q=q),
                                       ACT.Relu).then_inc(S["h2_hi"], 1)

                seen = 0
                for n, job in enumerate(LSTM):
                    p, _, _, s = job
                    w = width(job)
                    before = last_user(n)
                    for g_n, g in enumerate(gates_of(job)):
                        act.wait_ge(S["gate_full"], GATES * i + seen + g_n + 1)
                        if g_n == 0 and before is not None:
                            act.wait_ge(S["h_ready"], NL * i + before + 1)
                        a = act.activation(gates[:, s, g, 0:w], bank(n, g)[:, 0:w],
                                           ACT.Tanh if g == GG else ACT.Sigmoid,
                                           bias=lbias[:, 0, p - 1, g:g + 1])
                        a.then_inc(S["gate_act"], 1)
                    seen += len(gates_of(job))
                    act.wait_ge(S["cell_ready"], NL * i + n + 1)
                    act.activation(gates[:, s, GG, 0:w], cell[:, s, 0:w], ACT.Tanh).then_inc(S["tanh_done"], 1)

                for b in range(G):
                    act.wait_ge(S["x1_norm"], 4 * i + b + 1)
                    if b == 0:
                        act.wait_ge(S["out_full"], 4 * i + 1)
                    act.activation(buf_c[:, HI, b, :], res[:, b, :, :].rearrange("p c d -> p (c d)"),
                                   ACT.Copy).then_inc(S["x1_hi"], 1)
                for b in range(G):
                    act.wait_ge(S["gx_full"], 4 * i + b + 1)
                    act.activation(buf_d[:, HI, b, :], bank("GX", b), ACT.Copy).then_inc(S["gx_hi"], 1)
                for k in range(4):
                    act.wait_ge(S["qv_full"], 4 * i + k + 1)
                    act.activation(hn[:, k, :], bank("QV", k), ACT.Copy).then_inc(S["q_copied" if k < 2 else "v_copied"], 1)
                act.wait_ge(S["shifted"], i + 1)
                act.activation(sm[:, 2, :], sm[:, 0, :], ACT.Exp).then_inc(S["exp_done"], 1)
                for k in range(2):
                    act.wait_ge(S["m_ready"], 2 * i + k + 1)
                    act.activation(buf_c[:, HI, k, :], hn[:, 2 + k, :], ACT.Copy).then_inc(S["m_hi"], 1)
                for k in range(EC):
                    act.wait_ge(S["mw_full"], 2 * i + k + 1)
                    act.activation(buf_c[:, HI, 2 + k, :], bank("MW", k), ACT.Copy).then_inc(S["mw_hi"], 1)

        @block.vector
        def _(dve):
            chain = [0]

            def link(ins):
                chain[0] += 1
                ins.then_inc(S["dve_chain"], 1)
                dve.wait_ge(S["dve_chain"], chain[0])

            TT, TS = dve.tensor_tensor, dve.tensor_scalar
            dve.wait_ge(S["ld_edge"], 32)
            dve.wait_ge(S["ld_const"], 64)
            dve.wait_ge(S["ld_b"], 80)
            row = tmp[0:1, 0:2 * E]
            link(dve.tensor_copy(edge_f[:, :], edge_i[:, :]))
            link(dve.tensor_copy(row, edgerow_i[:, 0:2 * E]))
            key = small[:, 2:4]
            for c in range(EC):
                link(TS(key[:, c:c + 1], edge_f[:, c:c + 1], float(E), None, ALU.mult))
                link(TT(key[:, c:c + 1], key[:, c:c + 1], C(C_EDGE + c, C_EDGE + c + 1), ALU.add))
            link(TS(row[:, 0:E], row[:, 0:E], float(E), None, ALU.mult))
            TT(row[:, 0:E], row[:, 0:E], C(C_IOTA, C_IOTA + E)[0:1, :], ALU.add).then_inc(S["setup_dve"], 1)
            link(TT(lbias[:, 0, :, :], lbias[:, 0, :, :], lbias[:, 1, :, :], ALU.add))
            link(TS(a_blk[:, :, :], a_blk[:, :, :], small[:, 1:2], None, ALU.mult))
            dve.wait_ge(S["setup_pe"], 1)
            perm = tmp[:, 512:1024].rearrange("p (c r) -> p c r", c=EC)
            rank = small[:, 4:6]
            for c in range(EC):
                link(TS(tmp[:, 0:E], ps[:, 0, 0:E], key[:, c:c + 1], None, ALU.is_lt))
                link(dve.reduce_sum(rank[:, c:c + 1], tmp[:, 0:E], AX.X))
                link(TS(perm[:, c, :], C(C_IOTA, C_IOTA + E), rank[:, c:c + 1], None, ALU.is_equal))
            spread = tmp[:, 0:512].rearrange("p (k n) -> p k n", k=4)
            for k in range(4):
                link(TS(spread[:, k, :], C(C_ONES, C_ONES + 128), edge_f[:, k:k + 1], None, ALU.mult))
            dve.tensor_copy(b1_t[:, :], ps[:, 1, 0:D]).then_inc(S["setup_dve"], 1)
            dve.wait_ge(S["setup_pe"], 2)
            dve.wait_ge(S["setup_act"], 3)
            TT(adj_s[:, LO, :, :], raw_adj, adj_s[:, HI, :, :].bitcast(f32), ALU.subtract).then_inc(S["setup_dve"], 1)
            flat = lambda t, hl: t[:, hl, :, :].rearrange("p a n -> p (a n)")
            link(TT(flat(wg_s, LO), w_raw[:, 0:2 * D], flat(wg_s, HI).bitcast(f32), ALU.subtract))
            link(TT(flat(wa_s, LO), w_raw[:, 2 * D:5 * D], flat(wa_s, HI).bitcast(f32), ALU.subtract))
            for c in range(NC):
                node = C(C_NODE + c, C_NODE + c + 1)
                link(TS(sel_g[:, c, E:2 * E], ps[:, 2, E:2 * E], node, None, ALU.is_equal))
                link(dve.scalar_tensor_tensor(sel_g[:, c, 0:E], ps[:, 2, 0:E], node,
                                              sel_g[:, c, E:2 * E].bitcast(f32), ALU.is_equal, ALU.add))
            link(dve.tensor_copy(small[:, 6:8], ps[:, 3, 0:EC]))
            for c in range(EC):
                link(TS(sel_s[:, c, :], C(C_NROW, C_NROW + T), small[:, 6 + c:7 + c], None, ALU.is_equal))
            link(dve.tensor_copy(sm[:, 0, :], ps[0:16, 2, 0:E]))
            dve.wait_ge(S["setup_pool"], 4)
            link(TT(seg[:, 0, 1:E], sm[:, 0, 1:E], sm[:, 0, 0:E - 1], ALU.is_equal))
            link(TT(seg[:, 1, 0:E - 1], sm[:, 0, 1:E], sm[:, 0, 0:E - 1], ALU.is_equal))
            for k in range(2):
                link(TS(seg[:, 2 + k, :], seg[:, k, :], FAR, -FAR, ALU.mult, ALU.add))
            dve.wait_ge(S["setup_pe"], 3)
            link(TS(br_t[:, :], ps[:, 7, :], small[:, 0:1], None, ALU.mult))
            dve.tensor_copy(small[:, 8:10], small[:, 6:8]).then_inc(S["setup_dve"], 1)
            for c in range(EC):
                dve.wait_ge(S["setup_pe"], 4 + c)
                link(TT(tmp[:, 0:T], ps[:, 4 + c, :], sel_s[:, c, :].bitcast(f32), ALU.mult))
                link(dve.reduce_sum(small[:, 10 + c:11 + c], tmp[:, 0:T], AX.X))
                link(TS(tmp[:, 512 + 16 * c:528 + 16 * c], C(C_ONES, C_ONES + 16), small[:, 10 + c:11 + c], None, ALU.mult))
            dve.tensor_copy(small[:, 12:14], small[:, 6:8]).then_inc(S["setup_dve"], 1)
            dve.wait_ge(S["setup_act"], 5)
            for m in range(2):
                link(TT(wl_s[:, LO, m, :, :], lw_raw[:, m, :, :], wl_s[:, HI, m, :, :].bitcast(f32), ALU.subtract))
            dve.wait_ge(S["setup_act"], 6)
            for n, name in enumerate(("start", "z2_full", "hn_ready", "out_full", "out_summed")):
                dve.tensor_copy(small[:, 16 + n:17 + n], small[:, 6:7]).then_inc(S[name], 1)
            base = chain[0]

            def normalise(k):
                for m in range(G * NC):
                    link_last = dve.bn_stats(stats[:, m, :], res[:, m // NC, m % NC, :])
                link(link_last)
                dve.tensor_copy(small[:, 14:15], stats[:, 0, 0:1])
                for m in range(G * NC):
                    link_last = dve.bn_aggr(mv[:, m, :], stats[:, m, :])
                link(link_last)
                TS(rstd[:, :], mv[:, :, 1], EPS, None, ALU.add).then_inc(S["var_ready"], 1)
                dve.wait_ge(S["rstd_ready"], 2 * i + k + 1)
                for m in range(G * NC):
                    v = res[:, m // NC, m % NC, :]
                    ins = TS(v, v, mv[:, m, 0:1], rstd[:, m:m + 1], ALU.subtract, ALU.mult)
                    if k == 0 and m % NC == NC - 1:
                        ins.then_inc(S["x1_norm"], 1)
                    if k == 1 and m == G * NC - 1:
                        ins.then_inc(S["out_ready"], 1)

            with dve.Fori(0, ITERS) as i:
                count = [0]

                def link(ins):
                    count[0] += 1
                    ins.then_inc(S["dve_chain"], 1)
                    dve.wait_ge(S["dve_chain"], DVE_LINKS * i + base + count[0])

                for b in range(G):
                    dve.wait_ge(S["x_hi"], 4 * i + b + 1)
                    TT(buf_a[:, LO, b, :], x_in[:, b % 2, :, :].rearrange("p c d -> p (c d)"),
                       buf_a[:, HI, b, :].bitcast(f32), ALU.subtract).then_inc(S["x_ready"], 1)
                for b in range(G):
                    dve.wait_ge(S["u_hi"], 4 * i + b + 1)
                    TT(buf_b[:, LO, b, :], bank("U", b), buf_b[:, HI, b, :].bitcast(f32),
                       ALU.subtract).then_inc(S["u_ready"], 1)

                def add_bias(job, full, done, bias):
                    for b in range(G):
                        dve.wait_ge(S[full], 4 * i + b + 1 + (full == "z2_full"))
                        v = bank(job, b)
                        if job == "Z2":
                            v = v.rearrange("p (c h) -> p c h", h=D)
                        TT(v, v, bias, ALU.add).then_inc(S[done], 1)

                add_bias("Z", "z_full", "z_sum", br_t[:, :])
                for b in range(G):
                    dve.wait_ge(S["z_hi"], 4 * i + b + 1)
                    dve.scalar_tensor_tensor(buf_a[:, LO, b, :], bank("Z", b), 0.0, buf_a[:, HI, b, :].bitcast(f32),
                                             ALU.max, ALU.subtract).then_inc(S["h1_ready"], 1)
                add_bias("Z2", "z2_full", "z2_sum", b1_t[:, :].unsqueeze(1).broadcast_to([128, NC, D]))
                for b in range(G):
                    dve.wait_ge(S["z2_hi"], 4 * i + b + 1)
                    TT(buf_b[:, LO, b, :], bank("Z2", b), buf_b[:, HI, b, :].bitcast(f32),
                       ALU.subtract).then_inc(S["z2_ready"], 1)
                for b in range(G):
                    dve.wait_ge(S["h2_hi"], 8 * i + 2 * b + 2)
                    for r0, r1, c, q in pieces(b):
                        dve.scalar_tensor_tensor(h_t[:, LO, r0:r1, b, 0:q],
                                                 bank("H2", b)[:, c].rearrange("p (r q) -> p r q", q=q), 0.0,
                                                 h_t[:, HI, r0:r1, b, 0:q].bitcast(f32),
                                                 ALU.max, ALU.subtract).then_inc(S["h2_ready"], 1)

                seen = 0
                for n, job in enumerate(LSTM):
                    p, t, k, s = job
                    w = width(job)
                    g = gates[:, s, :, 0:w]
                    c = cell[:, s, 0:w]
                    dve.wait_ge(S["gate_act"], GATES * i + seen + 2)
                    if t == 0:
                        TT(c, g[:, GI, :], g[:, GG, :], ALU.mult).then_inc(S["cell_ready"], 1)
                    else:
                        TT(g[:, GI, :], g[:, GI, :], g[:, GG, :], ALU.mult)
                        dve.wait_ge(S["gate_act"], GATES * i + seen + 3)
                        link(TT(c, g[:, GF, :], c, ALU.mult))
                        TT(c, c, g[:, GI, :], ALU.add).then_inc(S["cell_ready"], 1)
                    seen += len(gates_of(job))
                    dve.wait_ge(S["tanh_done"], NL * i + n + 1)
                    link(TT(g[:, GF, :], g[:, GO, :], g[:, GG, :], ALU.mult))
                    if t == p - 1:
                        hi, lo, h = toks(HI, job), toks(LO, job), cols(gates[:, s, GF, :], job)
                    else:
                        hi, lo, h = rec[:, s, HI, 0:w], rec[:, s, LO, 0:w], g[:, GF, :]
                    link(dve.tensor_copy(hi, h))
                    TT(lo, h, hi.bitcast(f32), ALU.subtract).then_inc(S["h_ready"], 1)

                dve.wait_ge(S["h_ready"], NL * i + NL)
                for r0, r1, cc, q in pieces(0):
                    for b in range(G):
                        src = [h_t[:, hl, r0:r1, b, 0:q].bitcast(f32) for hl in (HI, LO)]
                        ins = TT(hn[:, b, cc].rearrange("p (r q) -> p r q", q=q), src[0], src[1], ALU.add)
                    ins.then_inc(S["hn_ready"], 1)
                dve.wait_ge(S["ld_res"], 16 * i + 16)
                for b in range(G):
                    dve.wait_ge(S["n_full"], 4 * i + b + 1)
                    v = res[:, b, :, :].rearrange("p c d -> p (c d)")
                    ins = TT(v, v, bank("N", b), ALU.add)
                    if b == G - 1:
                        ins.then_inc(S["n_summed"], 1)
                        dve.wait_ge(S["n_summed"], i + 1)
                normalise(0)
                for b in range(G):
                    dve.wait_ge(S["gx_hi"], 4 * i + b + 1)
                    TT(buf_d[:, LO, b, :], bank("GX", b), buf_d[:, HI, b, :].bitcast(f32),
                       ALU.subtract).then_inc(S["gx_ready"], 1)
                for k in range(2):
                    dve.wait_ge(S["q_copied"], 2 * i + k + 1)
                    dve.scalar_tensor_tensor(hn[:, k, :], hn[:, k, :], SLOPE, hn[:, k, :], ALU.mult, ALU.max)\
                       .then_inc(S["lrelu_ready"], 1)
                dve.wait_ge(S["sc_full"], i + 1)
                s0, s1, s2 = (sm[:, k, :] for k in range(3))
                link(TT(s0, bank("SC", 0)[0:16, 0:E], log_b[:, :], ALU.add))
                link(dve.tensor_tensor_scan(s1, seg[:, 2, :], s0, 0.0, ALU.add, ALU.max))
                link(dve.tensor_tensor_scan(s2[:, ::-1], seg[:, 3, ::-1], s1[:, ::-1], 0.0, ALU.add, ALU.max))
                TT(s0, s0, s2, ALU.subtract).then_inc(S["shifted"], 1)
                dve.wait_ge(S["exp_done"], i + 1)
                link(dve.tensor_tensor_scan(s1, seg[:, 0, :], s2, 0.0, ALU.mult, ALU.add))
                link(dve.tensor_tensor_scan(s0[:, ::-1], seg[:, 1, ::-1], s1[:, ::-1], 0.0, ALU.mult, ALU.max))
                link(dve.reciprocal(s0, s0))
                TT(s0, s0, s2, ALU.mult).then_inc(S["attn_ready"], 1)
                for k in range(2):
                    dve.wait_ge(S["ab_full"], 2 * i + k + 1)
                    if k == 0:
                        dve.wait_ge(S["v_copied"], 2 * i + 2)
                    TT(hn[:, 2 + k, :], hn[:, 2 + k, :], bank(f"AB{k}", 0), ALU.mult).then_inc(S["m_ready"], 1)
                for k in range(2):
                    dve.wait_ge(S["m_hi"], 2 * i + k + 1)
                    TT(buf_c[:, LO, k, :], hn[:, 2 + k, :], buf_c[:, HI, k, :].bitcast(f32),
                       ALU.subtract).then_inc(S["m_split"], 1)
                for k in range(EC):
                    dve.wait_ge(S["mw_hi"], 2 * i + k + 1)
                    TT(buf_c[:, LO, 2 + k, :], bank("MW", k), buf_c[:, HI, 2 + k, :].bitcast(f32),
                       ALU.subtract).then_inc(S["mw_ready"], 1)
                for c in range(NC):
                    dve.wait_ge(S["out_full"], 4 * i + c + 2)
                    ins = TT(res[:, :, c, :], res[:, :, c, :],
                             bank("OUT", c).rearrange("p (b d) -> p b d", b=G), ALU.add)
                ins.then_inc(S["out_summed"], 1)
                dve.wait_ge(S["out_summed"], i + 2)
                normalise(1)
                assert count[0] == DVE_LINKS

        @block.tensor
        def _(pe):
            mm = pe.matmul

            def exact3(o, l, r, start, stop):
                mm(o, l[HI], r[HI], start=start, stop=False)
                mm(o, l[HI], r[LO], start=False, stop=False)
                return mm(o, l[LO], r[HI], start=False, stop=stop)

            ones = C(C_ONES, C_ONES + 128)
            pe.wait_ge(S["setup_dve"], 1)
            mm(ps[:, 0, 0:E], ones[0:1, :], tmp[0:1, 0:E], start=True, stop=True)
            mm(ps[:, 1, 0:D], ones[0:1, :], b1_t[0:1, :], start=True, stop=True).then_inc(S["setup_pe"], 1)
            pe.wait_ge(S["setup_dve"], 2)
            perm = tmp[:, 512:1024].rearrange("p (c r) -> p c r", c=EC)
            spread = tmp[:, 0:512].rearrange("p (k n) -> p k n", k=4)
            for k in range(2):
                for c in range(EC):
                    mm(ps[:, 2, k * E:(k + 1) * E], spread[:, 2 * k + c, :], perm[:, c, :], start=(c == 0), stop=(c == EC - 1))
            for rc in range(EC):
                for c in range(EC):
                    m = mm(ps[:, 3, rc:rc + 1], perm[:, c, rc * 128:(rc + 1) * 128], edge_f[:, c:c + 1], start=(c == 0), stop=(c == EC - 1))
            m.then_inc(S["setup_pe"], 1)
            pe.wait_ge(S["setup_dve"], 3)
            pe.wait_ge(S["ones_r"], 1)
            for c in range(NC):
                for hl in (HI, LO):
                    m = mm(ps[:, 7, :], ones_r, adj_s[:, hl, c, :], start=(c == 0 and hl == HI), stop=(c == NC - 1 and hl == LO))
            m.then_inc(S["setup_pe"], 1)
            pe.wait_ge(S["setup_dve"], 4)
            for ec in range(EC):
                for c in range(NC):
                    for hl in (HI, LO):
                        m = mm(ps[:, 4 + ec, :], sel_g[:, c, E + ec * 128:E + (ec + 1) * 128], adj_s[:, hl, c, :],
                               start=(c == 0 and hl == HI), stop=(c == NC - 1 and hl == LO))
                m.then_inc(S["setup_pe"], 1)
            pe.wait_ge(S["setup_dve"], 5)
            for ec in range(EC):
                m = mm(ps[0:16, 6, ec * 128:(ec + 1) * 128], tmp[:, 512 + 16 * ec:528 + 16 * ec], ident[:, :], start=True, stop=True)
            m.then_inc(S["setup_pe"], 1)

            pe.wait_ge(S["start"], 1)
            with pe.Fori(0, ITERS) as i:
                def take(job):
                    n = JOBS.index(job)
                    if job == "Z":
                        pe.wait_ge(S["out_summed"], i + 1)
                    elif n >= 2:
                        name, per, count = READ_OUT[JOBS[n - 2]]
                        pe.wait_ge(S[name], per * i + count)

                take("U")
                for b in range(G):
                    pe.wait_ge(S["x_ready"], 4 * i + b + 1)
                    for c in range(NC):
                        m = exact3(bank("U", b), [buf_a[:, hl, b, c * 128:(c + 1) * 128] for hl in (HI, LO)],
                                   [adj_s[:, hl, c, :] for hl in (HI, LO)], c == 0, c == NC - 1)
                    m.then_inc(S["u_full"], 1)
                take("Z")
                for b in range(G):
                    pe.wait_ge(S["u_ready"], 4 * i + b + 1)
                    exact3(bank("Z", b), [wg_s[:, hl, 0, :] for hl in (HI, LO)],
                           [buf_b[:, hl, b, :] for hl in (HI, LO)], True, True).then_inc(S["z_full"], 1)
                take("Z2")
                for b in range(G):
                    pe.wait_ge(S["h1_ready"], 4 * i + b + 1)
                    for c in range(NC):
                        m = exact3(bank("Z2", b)[:, c * 128:(c + 1) * 128],
                                   [buf_a[:, hl, b, c * 128:(c + 1) * 128] for hl in (HI, LO)],
                                   [wg_s[:, hl, 1, :] for hl in (HI, LO)], True, True)
                    m.then_inc(S["z2_full"], 1)
                take("H2")
                for b in range(G):
                    pe.wait_ge(S["z2_ready"], 4 * i + b + 1)
                    for c in range(NC):
                        m = exact3(bank("H2", b), [buf_b[:, hl, b, c * 128:(c + 1) * 128] for hl in (HI, LO)],
                                   [adj_s[:, hl, c, :] for hl in (HI, LO)], c == 0, c == NC - 1)
                    m.then_inc(S["h2_full"], 1)

                pe.wait_ge(S["h2_ready"], 8 * i + 8)
                for n, job in enumerate(LSTM):
                    p, t, k, s = job
                    w = width(job)
                    take(n)
                    if p > 1 and t == 0:
                        pe.wait_ge(S["h_ready"], NL * i + done_before(n))
                    wi, wh = ([[wl_s[:, hl, m, p - 1, g * D:(g + 1) * D] for hl in (HI, LO)] for g in range(4)]
                              for m in range(2))
                    o = {g: cols(bank(n, g), job) for g in gates_of(job)}
                    for g in gates_of(job):
                        m = exact3(o[g], wi[g], [toks(hl, job) for hl in (HI, LO)], True, t == 0)
                        if t == 0:
                            m.then_inc(S["gate_full"], 1)
                    if t:
                        pe.wait_ge(S["h_ready"], NL * i + last_user(n) + 1)
                        for g in gates_of(job):
                            exact3(o[g], wh[g], [cols(rec[:, s, hl, :], job) for hl in (HI, LO)], False, True)\
                                .then_inc(S["gate_full"], 1)

                take("N")
                for b in range(G):
                    if b == 0:
                        pe.wait_ge(S["hn_ready"], 2 * i + 3)
                    for c in range(NC):
                        m = pe.transpose(bank("N", b)[:, c * 128:(c + 1) * 128], hn[:, b, c * 128:(c + 1) * 128], ident[:, :])
                    m.then_inc(S["n_full"], 1)
                take("GX")
                for b in range(G):
                    pe.wait_ge(S["x1_ready"], 4 * i + b + 1)
                    for c in range(NC):
                        for hl in (HI, LO):
                            m = mm(bank("GX", b), buf_c[:, hl, b, c * 128:(c + 1) * 128], sel_g[:, c, :],
                                   start=(c == 0 and hl == HI), stop=(c == NC - 1 and hl == LO))
                    m.then_inc(S["gx_full"], 1)
                take("QV")
                pe.wait_ge(S["gx_ready"], 4 * i + 4)
                for k in range(4):
                    m, b = k // 2, 2 * (k % 2)
                    exact3(bank("QV", k).rearrange("p (b e) -> p b e", b=2), [wa_s[:, hl, m, :] for hl in (HI, LO)],
                           [buf_d[:, hl, b:b + 2, m * E:(m + 1) * E] for hl in (HI, LO)], True, True)\
                        .then_inc(S["qv_full"], 1)
                take("SC")
                pe.wait_ge(S["lrelu_ready"], 2 * i + 2)
                for b in range(G):
                    m = mm(bank("SC", 0)[0:16, 0:E], a_blk[:, b, :], hn[:, b // 2, (b % 2) * E:(b % 2 + 1) * E],
                           start=(b == 0), stop=(b == G - 1))
                m.then_inc(S["sc_full"], 1)
                for k in range(2):
                    take(f"AB{k}")
                    if k == 0:
                        pe.wait_ge(S["attn_ready"], i + 1)
                    for b in range(2):
                        m = mm(bank(f"AB{k}", 0)[:, b * E:(b + 1) * E], eall[:, 2 * k + b, :], sm[:, 0, :], start=True, stop=True)
                    m.then_inc(S["ab_full"], 1)
                take("MW")
                pe.wait_ge(S["m_split"], 2 * i + 2)
                for ec in range(EC):
                    for b in range(G):
                        c0 = (b % 2) * E + ec * 128
                        m = exact3(bank("MW", ec)[:, b * D:(b + 1) * D],
                                   [buf_c[:, hl, b // 2, c0:c0 + 128] for hl in (HI, LO)],
                                   [wa_s[:, hl, 2, :] for hl in (HI, LO)], True, True)
                    m.then_inc(S["mw_full"], 1)
                take("OUT")
                pe.wait_ge(S["mw_ready"], 2 * i + 2)
                for c in range(NC):
                    for ec in range(EC):
                        for hl in (HI, LO):
                            m = mm(bank("OUT", c), sel_s[:, ec, c * 128:(c + 1) * 128], buf_c[:, hl, 2 + ec, :],
                                   start=(ec == 0 and hl == HI), stop=(ec == EC - 1 and hl == LO))
                    m.then_inc(S["out_full"], 1)


def kernel(x, adj, L0_gnn_Wg0, L0_gnn_bg0, L0_gnn_Wg1, L0_gnn_bg1, L0_gnn_Wih, L0_gnn_Whh, L0_gnn_bih,
           L0_gnn_bhh, L1_gnn_W_lin, L1_gnn_W_val, L1_gnn_a, L1_gnn_W_out, L1_gnn_src, L1_gnn_dst):
    import numpy as np
    import concourse.bacc as bacc
    from concourse.bass_utils import run_bass_kernel_spmd

    order = np.concatenate([np.arange(r, T, R) for r in range(R)])
    place = np.argsort(order)

    consts = np.zeros((128, C_END), np.float32)
    consts[:, C_ID:C_ID + 128] = np.eye(128)
    d, col = np.arange(128)[:, None], np.arange(16)[None, :]
    for b in range(G):
        consts[:, C_MASK + 16 * b:C_MASK + 16 * b + 16] = col == HEADS * b + d // (D // HEADS)
        consts[0:16, C_EALL + 128 * b:C_EALL + 128 * b + 128] = (col == HEADS * b + d // (D // HEADS)).T
    consts[:, C_NODE:C_NODE + NC] = order.reshape(NC, 128).T
    consts[:, C_NROW:C_NROW + T] = order
    consts[:, C_IOTA:C_IOTA + E] = np.arange(E)
    consts[:, C_EDGE:C_EDGE + EC] = np.arange(E).reshape(EC, 128).T
    consts[:, C_ONES:C_ONES + 128] = 1.0

    X = np.asarray(x)[:, order, :].reshape(ITERS, G, NC, 128, D).transpose(0, 3, 1, 2, 4)
    A = np.asarray(adj)[order][:, order].T.reshape(NC, 128, T).transpose(1, 0, 2)
    src, dst = np.asarray(L1_gnn_src), np.asarray(L1_gnn_dst)
    cols = np.concatenate([src.reshape(EC, 128), dst.reshape(EC, 128)]).T
    rows = np.concatenate([src, dst])[None, :]
    stack = lambda ws: np.concatenate([np.asarray(w) for w in ws], axis=1)
    gate_cols = lambda w: np.asarray(w).transpose(2, 0, 1)
    bias = lambda v: np.asarray(v).reshape(SKIPS, 4, D).transpose(2, 0, 1)
    arrays = {
        "x": X, "adjT": A, "consts": consts, "edge_col": cols, "edge_row": rows,
        "w_gnn": stack([L0_gnn_Wg0, L0_gnn_Wg1, np.asarray(L1_gnn_W_lin).T, np.asarray(L1_gnn_W_val).T,
                        np.asarray(L1_gnn_W_out).T]),
        "b_gnn0": np.asarray(L0_gnn_bg0)[:, None], "b_gnn1": np.asarray(L0_gnn_bg1)[None, :],
        "w_ih": gate_cols(L0_gnn_Wih), "w_hh": gate_cols(L0_gnn_Whh),
        "b_ih": bias(L0_gnn_bih), "b_hh": bias(L0_gnn_bhh),
        "a_col": np.asarray(L1_gnn_a).reshape(D, 1),
    }
    arrays = {k: np.ascontiguousarray(v) for k, v in arrays.items()}
    nc = bacc.Bacc("TRN2", target_bir_lowering=False, num_devices=1)
    args = {k: nc.dram_tensor(k, v.shape, mybir.dt.from_np(v.dtype), kind="ExternalInput").ap()
            for k, v in arrays.items()}
    out = nc.dram_tensor("out", (ITERS, 128, G, NC, D), mybir.dt.float32, kind="ExternalOutput").ap()
    build(nc, out=out, **args)
    r = run_bass_kernel_spmd(nc, [arrays], core_ids=[0])
    y = r.results[0]["out"].transpose(0, 2, 3, 1, 4).reshape(B, T, D)
    return np.ascontiguousarray(y[:, place, :])
```

```python
import concourse.bass as bass
from concourse import mybir
from contextlib import ExitStack

B, T, D = 16, 512, 128
G = 4
ITERS = B // G
NC = T // 128
HEADS, E = 4, 256
EC = E // 128
SKIPS = 4
R, Q = 12, 43
RFULL = T - R * (Q - 1)
CUT = RFULL * Q
W = 2 * G * Q
W4 = 3 * (G // 2) * Q
EPS = 1e-5
LOG_EPS = 1e-8
SLOPE = 0.2
FAR = 3e38
GI, GF, GG, GO = range(4)

C_ID, C_MASK, C_NODE, C_NROW, C_IOTA, C_EDGE, C_ONES, C_EALL, C_END = (
    0, 128, 192, 196, 708, 964, 966, 1094, 1606)


def lstm_jobs():
    jobs = [(1, 0, s, s % 3) for s in range(6)]
    for p, chunks in ((2, 3), (3, 2), (4, 2)):
        jobs += [(p, t, k, k) for t in range(p) for k in range(chunks)]
    return jobs


LSTM = lstm_jobs()
NL = len(LSTM)


def width(job):
    return W4 if job[0] == 4 else W


def gates_of(job):
    return [GI, GG, GO] if job[1] == 0 else [GI, GG, GF, GO]


def done_before(n):
    p, t, k, _ = LSTM[n]
    if p == 1:
        return 0
    last = {2: (1, 0, 2 * k + 1), 3: (2, 1, k + 1), 4: (3, 2, 1)}[p]
    return 1 + next(m for m, j in enumerate(LSTM) if j[:3] == last)


def last_user(n):
    return next((m for m in range(n - 1, -1, -1) if LSTM[m][3] == LSTM[n][3]), None)


GATES = sum(len(gates_of(j)) for j in LSTM)


def gates_before(n):
    return sum(len(gates_of(j)) for j in LSTM[:n])


GNN_FIRST = ["X0", "X1", "U0", "U1", "Z0", "Z1", "Y0", "Y1", "H0", "H1"]
ATTENTION = ["S0", "A0", "S1", "A1", "GX0", "GX1", "Q", "V", "SC", "AB0", "AB1", "MW", "O0", "O1",
             "T0", "F0", "T1", "F1"]
BODY_TEXT = """
    0 X0+ 1 S0- 2 U0+ 3 A0- X1+ 4 S1- 5 U1+
    6 A1- GX0- 7 Z0+ 8 GX1- 9 Z1+ 10 Q- 11 V-
    12 Y0+ 13 SC- 14 Y1+ 15 AB0- 16 AB1- 17 MW-
    18 O0- 19 O1- 20 T0- 21 F0- T1- 22 F1- 23 24 25
    H0+ K H1+ N0 N1
"""


def parse(text):
    jobs = []
    for word in text.split():
        offset = {"+": 1, "-": -1}.get(word[-1], 0)
        name = word.rstrip("+-")
        jobs.append((int(name) if name.isdigit() else name, offset))
    return jobs


BODY = parse(BODY_TEXT)
assert sorted(map(str, [j for j, _ in BODY])) == sorted(map(str, GNN_FIRST + ATTENTION + ["K", "N0", "N1"] + list(range(NL))))


def body(i):
    return [(job, i + off) for job, off in BODY if 0 <= i + off < ITERS]


BEFORE = [(job, 0) for job in GNN_FIRST]
AFTER = [(job, ITERS - 1) for job in ATTENTION]
NO_PSUM = {"X0", "X1", "K", "S0", "S1", "A0", "A1", "T0", "T1", "F0", "F1"}

ORDER = [j for j in BEFORE + [j for i in range(ITERS) for j in body(i)] + AFTER if j[0] not in NO_PSUM]
HALF = {j: n % 2 for n, j in enumerate(ORDER)}
HELD_BY = {j: ORDER[n - 2] if n >= 2 else None for n, j in enumerate(ORDER)}
for _job, _off in BODY:
    if _job not in NO_PSUM:
        (_a, _b), _c = ((_job, 1 + _off), (_job, 2 + _off)), None
        assert HALF[_a] == HALF[_b] and HELD_BY[_b] == (HELD_BY[_a][0], HELD_BY[_a][1] + 1)

READ_OUT = {"SC": ("shifted", 1, 1), "Q": ("lrelu_ready", 2, 2), "V": ("v_copied", 2, 2), "MW": ("mw_ready", 2, 2)}
for _k in range(2):
    READ_OUT.update({f"U{_k}": ("u_ready", 4, 2 * _k + 2), f"Z{_k}": ("h1_ready", 4, 2 * _k + 2),
                     f"Y{_k}": ("z2_ready", 4, 2 * _k + 2), f"H{_k}": ("h2_ready", 8, 4 * _k + 4),
                     f"N{_k}": ("n_summed", 2, _k + 1), f"GX{_k}": ("gx_ready", 4, 2 * _k + 2),
                     f"AB{_k}": ("m_ready", 2, _k + 1), f"O{_k}": ("out_summed", 2, _k + 1)})
READ_OUT.update({n: ("gate_act", GATES, gates_before(n + 1)) for n in range(NL)})

DVE_LINKS = 79


def build(nc, x, adjT, consts, edge_col, edge_row, w_gnn, b_gnn0, b_gnn1, w_ih, w_hh, b_ih, b_hh,
          a_col, out):
    f32, f32r, i32 = mybir.dt.float32, mybir.dt.float32r, mybir.dt.int32
    ALU, ACT, AX = mybir.AluOpType, mybir.ActivationFunctionType, mybir.AxisListType
    HI, LO = 0, 1

    ctx = ExitStack()
    with ctx:
        def sb(name, shape, dt=f32):
            return ctx.enter_context(nc.sbuf_tensor(name, shape, dt))

        def sem(name):
            return ctx.enter_context(nc.semaphore(name))

        adj_s = sb("adj_s", [128, 2, NC, T], f32r)
        wg_s = sb("wg_s", [128, 2, 2, D], f32r)
        wa_s = sb("wa_s", [128, 2, 3, D], f32r)
        wl_s = sb("wl_s", [128, 2, 2, SKIPS, 4 * D], f32r)
        sel_g = sb("sel_g", [128, NC, 2 * E], f32r)
        sel_s = sb("sel_s", [128, EC, T], f32r)
        br_t = sb("br_t", [128, T])
        b1_t = sb("b1_t", [128, D])
        lbias = sb("lbias", [128, 2, SKIPS, 4])
        ident = sb("ident", [128, 128])
        eall = sb("eall", [16, G, 128])
        a_blk = sb("a_blk", [128, G, 16])
        log_b = sb("log_b", [16, E])
        seg = sb("seg", [16, 4, E])
        half_c = sb("half_c", [128, 1])
        eps8 = sb("eps8", [128, 1])

        x_in = sb("x_in", [128, 2, NC, D])
        buf_a = sb("buf_a", [128, 2, G, T], f32r)
        buf_b = sb("buf_b", [128, 2, G, T], f32r)
        h_t = sb("h_t", [128, 2, R, G, Q], f32r)
        gates = sb("gates", [128, 3, 4, W])
        cell = sb("cell", [128, 3, W])
        rec = sb("rec", [128, 3, 2, W], f32r)
        hn = sb("hn", [128, G, T])
        res = sb("res", [128, G, NC, D])
        buf_c = sb("buf_c", [128, 2, G, T], f32r)
        buf_d = sb("buf_d", [128, 2, G, T], f32r)
        stats = sb("stats", [128, G * NC, 6])
        mv = sb("mv", [128, G * NC, 2])
        rstd = sb("rstd", [128, G * NC])
        sm = sb("sm", [16, 3, E])

        ps = ctx.enter_context(nc.psum_tensor("ps", [128, 8, 512], f32))

        names = ("ld_x0 ld_x1 ld_res0 ld_res1 ld_adj ld_const ld_edge ld_w ld_lw ld_b st_out0 st_out1 "
                 "setup_dve setup_pe setup_act setup_pool start "
                 "x_hi x_ready u_full u_hi u_ready z_full z_sum z_hi h1_ready z2_full z2_sum z2_hi z2_ready "
                 "h2_full h2_hi h2_ready gate_full gate_act cell_ready tanh_done h_ready "
                 "hn_ready n_full var_ready rstd_ready x1_norm x1_hi x1_ready gx_full gx_hi gx_ready "
                 "q_full q_scaled v_full v_copied lrelu_ready sc_full shifted exp_done attn_ready ab_full "
                 "m_ready m_hi m_split mw_full mw_hi mw_ready out_full out_ready "
                 "n_summed out_summed ones_r dve_chain").split()
        S = {n: sem(n) for n in names}

        block = ctx.enter_context(nc.Block())

        def need(eng, name, value):
            if not isinstance(value, int) or value > 0:
                eng.wait_ge(S[name], value)

        def in_order(eng, handle):
            for job, g in BEFORE + body(0):
                handle(job, g, g)
            with eng.Fori(1, ITERS - 1) as i:
                for job, off in BODY:
                    handle(job, i + off, 1 + off)
            for job, g in body(ITERS - 1) + AFTER:
                handle(job, g, g)

        def bank(job, like, n):
            return ps[:, 4 * HALF[job, like] + n, :]

        def flat(ap):
            return ap.rearrange("p c d -> p (c d)")

        PAIR = {f"{name}{k}": (2 * k, 2 * k + 1) for name in "X U Z Y H N S A GX T F O".split() for k in range(2)}

        def toks(hl, job, step=None):
            p, t, k, _ = job
            t = t if step is None else step
            if p == 1:
                return h_t[:, hl, 2 * k:2 * k + 2, :, :].rearrange("p r b q -> p r (b q)")
            if p == 2:
                return h_t[:, hl, 4 * k + t:4 * k + t + 3:2, :, :].rearrange("p r b q -> p r (b q)")
            if p == 3:
                return h_t[:, hl, 6 * k + t:6 * k + t + 4:3, :, :].rearrange("p r b q -> p r (b q)")
            h = G // 2
            return h_t[:, hl, t:t + 9:4, h * k:h * k + h, :].rearrange("p r b q -> p r (b q)")

        def cols(ap, job):
            n = 3 if job[0] == 4 else 2
            return ap[:, 0:width(job)].rearrange("p (r c) -> p r c", r=n)

        def pieces(b):
            for r0, r1, c0, c1, q in ((0, RFULL, 0, CUT, Q), (RFULL, R, CUT, T, Q - 1)):
                yield r0, r1, slice(c0, c1), q

        sc = hn[:, :, :].rearrange("p b t -> p (b t)")
        w_raw = sc[:, 0:5 * D]
        cst = gates[:, :, :, :].rearrange("p a b c -> p (a b c)")
        raw_adj = res[:, :, :, :].rearrange("p c t d -> p c (t d)")
        tmp = sc[:, 1024:2048]
        lw_raw = cst[:, 0:4096].rearrange("p (a s n) -> p a s n", a=2, s=SKIPS)

        const_t = cell[:, :, :].rearrange("p s c -> p (s c)")[:, 0:C_EALL - C_NODE]
        def C(a, b):
            return const_t[:, a - C_NODE:b - C_NODE]
        edge_i = sb("edge_i", [128, 4], i32)
        edgerow_i = x_in[0:1, 0, :, :].rearrange("p c d -> p (c d)").bitcast(i32)
        edge_f = sb("edge_f", [128, 4])
        small = sb("small", [128, 24])
        ones_r = rec[:, 0, HI, 0:128]

        @block.sync
        def _(sp):
            sp.dma_start(raw_adj, adjT).then_inc(S["ld_adj"], 16)
            sp.dma_start(w_raw, w_gnn).then_inc(S["ld_w"], 16)
            sp.dma_start(lw_raw[:, 0, :, :], w_ih).then_inc(S["ld_lw"], 16)
            sp.dma_start(lw_raw[:, 1, :, :], w_hh).then_inc(S["ld_lw"], 16)
            def load_x(it):
                for b in range(G):
                    if G * it + b >= 2:
                        sp.wait_ge(S["x_ready"], G * it + b - 1)
                    elif b == 0:
                        sp.wait_ge(S["setup_dve"], 1)
                    sp.dma_start(x_in[:, b % 2, :, :], x[it, :, b]).then_inc(S[f"ld_x{b % 2}"], 16)

            load_x(0)
            sp.wait_ge(S["start"], 1)
            for it in range(ITERS):
                if it + 1 < ITERS:
                    load_x(it + 1)
                for k in range(2):
                    pair = slice(2 * k, 2 * k + 2)
                    if it:
                        sp.wait_ge(S["out_ready"], 2 * (it - 1) + k + 1)
                        sp.dma_start(out[it - 1, :, pair], res[:, pair, :, :]).then_inc(S[f"st_out{k}"], 16)
                        sp.wait_ge(S[f"st_out{k}"], 16 * it)
                    sp.dma_start(res[:, pair, :, :], x[it, :, pair]).then_inc(S[f"ld_res{k}"], 16)
            for k in range(2):
                pair = slice(2 * k, 2 * k + 2)
                sp.wait_ge(S["out_ready"], 2 * (ITERS - 1) + k + 1)
                sp.dma_start(out[ITERS - 1, :, pair], res[:, pair, :, :]).then_inc(S[f"st_out{k}"], 16)
            for k in range(2):
                sp.wait_ge(S[f"st_out{k}"], 16 * ITERS)

        @block.gpsimd
        def _(pool):
            pool.memset(half_c[:, :], -0.5).then_inc(S["setup_pool"], 1)
            pool.memset(eps8[:, :], LOG_EPS).then_inc(S["setup_pool"], 1)
            pool.memset(ones_r.bitcast(f32), 1.0).then_inc(S["ones_r"], 1)
            pool.memset(seg[:, :, :], 0.0).then_inc(S["setup_pool"], 1)
            pool.memset(h_t[:, :, :, :, :].bitcast(f32), 0.0).then_inc(S["setup_pool"], 1)

            def handle(job, i, like):
                if job in ("X0", "X1"):
                    for b in PAIR[job]:
                        pool.wait_ge(S["x_hi"], 4 * i + b + 1)
                        pool.tensor_tensor(buf_a[:, LO, b, :], flat(x_in[:, b % 2]), buf_a[:, HI, b, :].bitcast(f32),
                                           ALU.subtract).then_inc(S["x_ready"], 1)
                elif job == "K":
                    pool.wait_ge(S["h_ready"], NL * i + NL)
                    need(pool, "m_split", 2 * i)
                    for b in range(G):
                        for r0, r1, c, q in pieces(b):
                            hi, lo = (h_t[:, hl, r0:r1, b, 0:q].bitcast(f32) for hl in (HI, LO))
                            pool.tensor_tensor(hn[:, b, c].rearrange("p (r q) -> p r q", q=q), hi, lo, ALU.add)\
                                .then_inc(S["hn_ready"], 1)
                elif job in ("S0", "S1", "T0", "T1"):
                    k = int(job[1])
                    pool.wait_ge(S["var_ready"], 4 * i + 2 * (job[0] == "T") + k + 1)
                    r = rstd[:, 8 * k:8 * k + 8]
                    pool.tensor_tensor(r, r, half_c[:, 0:1].broadcast_to([128, 8]), ALU.pow)\
                        .then_inc(S["rstd_ready"], 1)
                elif job in ("A0", "A1"):
                    for b in PAIR[job]:
                        pool.wait_ge(S["x1_hi"], 4 * i + b + 1)
                        pool.tensor_tensor(buf_c[:, LO, b, :], flat(res[:, b]), buf_c[:, HI, b, :].bitcast(f32),
                                           ALU.subtract).then_inc(S["x1_ready"], 1)
                elif job in ("AB0", "AB1"):
                    k = int(job[2])
                    pool.wait_ge(S["m_hi"], 2 * i + k + 1)
                    pool.tensor_tensor(buf_c[:, LO, k, :], hn[:, 2 + k, :], buf_c[:, HI, k, :].bitcast(f32),
                                       ALU.subtract).then_inc(S["m_split"], 1)

            in_order(pool, handle)

        @block.scalar
        def _(act):
            act.dma_start(const_t, consts[:, C_NODE:C_EALL]).then_inc(S["ld_const"], 16)
            act.dma_start(ident[:, :], consts[:, C_ID:C_ID + 128]).then_inc(S["ld_const"], 16)
            act.dma_start(a_blk[:, :, :].rearrange("p b h -> p (b h)"),
                          consts[:, C_MASK:C_MASK + 64]).then_inc(S["ld_const"], 16)
            act.dma_start(eall[:, :, :].rearrange("p b h -> p (b h)"),
                          consts[0:16, C_EALL:C_EALL + 512]).then_inc(S["ld_const"], 16)
            act.dma_start(edge_i[:, :], edge_col).then_inc(S["ld_edge"], 16)
            act.dma_start(edgerow_i[:, 0:2 * E], edge_row).then_inc(S["ld_edge"], 16)
            act.dma_start(small[:, 0:1], b_gnn0).then_inc(S["ld_b"], 16)
            act.dma_start(small[:, 1:2], a_col).then_inc(S["ld_b"], 16)
            act.dma_start(lbias[:, 0, :, :], b_ih).then_inc(S["ld_b"], 16)
            act.dma_start(lbias[:, 1, :, :], b_hh).then_inc(S["ld_b"], 16)
            act.dma_start(b1_t[0:1, :], b_gnn1).then_inc(S["ld_b"], 16)
            act.wait_ge(S["ld_adj"], 16)
            act.activation(adj_s[:, HI, :, :], raw_adj, ACT.Copy).then_inc(S["setup_act"], 1)
            act.wait_ge(S["ld_w"], 16)
            act.activation(wg_s[:, HI, :, :].rearrange("p a n -> p (a n)"), w_raw[:, 0:2 * D], ACT.Copy).then_inc(S["setup_act"], 1)
            act.activation(wa_s[:, HI, :, :].rearrange("p a n -> p (a n)"), w_raw[:, 2 * D:5 * D], ACT.Copy).then_inc(S["setup_act"], 1)
            act.wait_ge(S["ld_lw"], 32)
            for m in range(2):
                act.activation(wl_s[:, HI, m, :, :], lw_raw[:, m, :, :], ACT.Copy).then_inc(S["setup_act"], 1)
            act.wait_ge(S["setup_pool"], 2)
            act.wait_ge(S["setup_pe"], 6)
            act.activation(log_b[:, :], ps[0:16, 6, 0:E], ACT.Ln, bias=eps8[0:16, :]).then_inc(S["setup_act"], 1)

            def handle(job, i, like):
                kind = job if isinstance(job, int) else job.rstrip("01")
                if kind == "X":
                    for b in PAIR[job]:
                        act.wait_ge(S[f"ld_x{b % 2}"], 32 * i + 16 * (b // 2) + 16)
                        need(act, "z2_full", 4 * i)
                        act.activation(buf_a[:, HI, b, :], flat(x_in[:, b % 2]), ACT.Copy).then_inc(S["x_hi"], 1)
                elif kind == "U":
                    for b in PAIR[job]:
                        act.wait_ge(S["u_full"], 4 * i + b + 1)
                        act.activation(buf_b[:, HI, b, :], bank(job, like, b % 2), ACT.Copy).then_inc(S["u_hi"], 1)
                elif kind == "Z":
                    for b in PAIR[job]:
                        act.wait_ge(S["z_sum"], 4 * i + b + 1)
                        act.activation(buf_a[:, HI, b, :], bank(job, like, b % 2), ACT.Relu).then_inc(S["z_hi"], 1)
                elif kind == "Y":
                    for b in PAIR[job]:
                        act.wait_ge(S["z2_sum"], 4 * i + b + 1)
                        act.activation(buf_b[:, HI, b, :], bank(job, like, b % 2), ACT.Copy).then_inc(S["z2_hi"], 1)
                elif kind == "H":
                    need(act, "hn_ready", 8 * i)
                    for b in PAIR[job]:
                        act.wait_ge(S["h2_full"], 4 * i + b + 1)
                        for r0, r1, c, q in pieces(b):
                            act.activation(h_t[:, HI, r0:r1, b, 0:q],
                                           bank(job, like, b % 2)[:, c].rearrange("p (r q) -> p r q", q=q),
                                           ACT.Relu).then_inc(S["h2_hi"], 1)
                elif isinstance(job, int):
                    p, _, _, s = LSTM[job]
                    w = width(LSTM[job])
                    before = last_user(job)
                    for n, g in enumerate(gates_of(LSTM[job])):
                        act.wait_ge(S["gate_full"], GATES * i + gates_before(job) + n + 1)
                        if n == 0 and before is not None:
                            act.wait_ge(S["h_ready"], NL * i + before + 1)
                        act.activation(gates[:, s, g, 0:w], bank(job, like, g)[:, 0:w],
                                       ACT.Tanh if g == GG else ACT.Sigmoid,
                                       bias=lbias[:, 0, p - 1, g:g + 1]).then_inc(S["gate_act"], 1)
                    act.wait_ge(S["cell_ready"], NL * i + job + 1)
                    act.activation(gates[:, s, GG, 0:w], cell[:, s, 0:w], ACT.Tanh).then_inc(S["tanh_done"], 1)
                elif kind == "A":
                    for b in PAIR[job]:
                        act.wait_ge(S["x1_norm"], 4 * i + b + 1)
                        need(act, "out_full", 4 * i)
                        act.activation(buf_c[:, HI, b, :], flat(res[:, b]), ACT.Copy).then_inc(S["x1_hi"], 1)
                elif kind == "GX":
                    for b in PAIR[job]:
                        act.wait_ge(S["gx_full"], 4 * i + b + 1)
                        act.activation(buf_d[:, HI, b, :], bank(job, like, b % 2), ACT.Copy).then_inc(S["gx_hi"], 1)
                elif kind == "Q":
                    for k in range(2):
                        act.wait_ge(S["q_full"], 2 * i + k + 1)
                        act.activation(hn[:, k, :], bank(job, like, k), ACT.Copy, scale=SLOPE).then_inc(S["q_scaled"], 1)
                elif kind == "V":
                    for k in range(2):
                        act.wait_ge(S["v_full"], 2 * i + k + 1)
                        act.activation(hn[:, 2 + k, :], bank(job, like, k), ACT.Copy).then_inc(S["v_copied"], 1)
                elif kind == "SC":
                    act.wait_ge(S["shifted"], i + 1)
                    act.activation(sm[:, 2, :], sm[:, 0, :], ACT.Exp).then_inc(S["exp_done"], 1)
                elif kind == "AB":
                    k = int(job[2])
                    act.wait_ge(S["m_ready"], 2 * i + k + 1)
                    act.activation(buf_c[:, HI, k, :], hn[:, 2 + k, :], ACT.Copy).then_inc(S["m_hi"], 1)
                elif kind == "MW":
                    for k in range(EC):
                        act.wait_ge(S["mw_full"], 2 * i + k + 1)
                        act.activation(buf_c[:, HI, 2 + k, :], bank(job, like, k), ACT.Copy).then_inc(S["mw_hi"], 1)

            in_order(act, handle)

        @block.vector
        def _(dve):
            chain = [0]

            def link(ins):
                chain[0] += 1
                ins.then_inc(S["dve_chain"], 1)
                dve.wait_ge(S["dve_chain"], chain[0])

            TT, TS = dve.tensor_tensor, dve.tensor_scalar
            dve.wait_ge(S["ld_edge"], 32)
            dve.wait_ge(S["ld_const"], 64)
            dve.wait_ge(S["ld_b"], 80)
            row = tmp[0:1, 0:2 * E]
            link(dve.tensor_copy(edge_f[:, :], edge_i[:, :]))
            link(dve.tensor_copy(row, edgerow_i[:, 0:2 * E]))
            key = small[:, 2:4]
            for c in range(EC):
                link(TS(key[:, c:c + 1], edge_f[:, c:c + 1], float(E), None, ALU.mult))
                link(TT(key[:, c:c + 1], key[:, c:c + 1], C(C_EDGE + c, C_EDGE + c + 1), ALU.add))
            link(TS(row[:, 0:E], row[:, 0:E], float(E), None, ALU.mult))
            TT(row[:, 0:E], row[:, 0:E], C(C_IOTA, C_IOTA + E)[0:1, :], ALU.add).then_inc(S["setup_dve"], 1)
            link(TT(lbias[:, 0, :, :], lbias[:, 0, :, :], lbias[:, 1, :, :], ALU.add))
            link(TS(a_blk[:, :, :], a_blk[:, :, :], small[:, 1:2], None, ALU.mult))
            dve.wait_ge(S["setup_pe"], 1)
            perm = tmp[:, 512:1024].rearrange("p (c r) -> p c r", c=EC)
            rank = small[:, 4:6]
            for c in range(EC):
                link(TS(tmp[:, 0:E], ps[:, 0, 0:E], key[:, c:c + 1], None, ALU.is_lt))
                link(dve.reduce_sum(rank[:, c:c + 1], tmp[:, 0:E], AX.X))
                link(TS(perm[:, c, :], C(C_IOTA, C_IOTA + E), rank[:, c:c + 1], None, ALU.is_equal))
            spread = tmp[:, 0:512].rearrange("p (k n) -> p k n", k=4)
            for k in range(4):
                link(TS(spread[:, k, :], C(C_ONES, C_ONES + 128), edge_f[:, k:k + 1], None, ALU.mult))
            dve.tensor_copy(b1_t[:, :], ps[:, 1, 0:D]).then_inc(S["setup_dve"], 1)
            dve.wait_ge(S["setup_pe"], 2)
            dve.wait_ge(S["setup_act"], 3)
            TT(adj_s[:, LO, :, :], raw_adj, adj_s[:, HI, :, :].bitcast(f32), ALU.subtract).then_inc(S["setup_dve"], 1)
            link(TT(flat(wg_s[:, LO]), w_raw[:, 0:2 * D], flat(wg_s[:, HI]).bitcast(f32), ALU.subtract))
            link(TT(flat(wa_s[:, LO]), w_raw[:, 2 * D:5 * D], flat(wa_s[:, HI]).bitcast(f32), ALU.subtract))
            for c in range(NC):
                node = C(C_NODE + c, C_NODE + c + 1)
                link(TS(sel_g[:, c, E:2 * E], ps[:, 2, E:2 * E], node, None, ALU.is_equal))
                link(dve.scalar_tensor_tensor(sel_g[:, c, 0:E], ps[:, 2, 0:E], node,
                                              sel_g[:, c, E:2 * E].bitcast(f32), ALU.is_equal, ALU.add))
            link(dve.tensor_copy(small[:, 6:8], ps[:, 3, 0:EC]))
            for c in range(EC):
                link(TS(sel_s[:, c, :], C(C_NROW, C_NROW + T), small[:, 6 + c:7 + c], None, ALU.is_equal))
            link(dve.tensor_copy(sm[:, 0, :], ps[0:16, 2, 0:E]))
            dve.wait_ge(S["setup_pool"], 4)
            link(TT(seg[:, 0, 1:E], sm[:, 0, 1:E], sm[:, 0, 0:E - 1], ALU.is_equal))
            link(TT(seg[:, 1, 0:E - 1], sm[:, 0, 1:E], sm[:, 0, 0:E - 1], ALU.is_equal))
            for k in range(2):
                link(TS(seg[:, 2 + k, :], seg[:, k, :], FAR, -FAR, ALU.mult, ALU.add))
            dve.wait_ge(S["setup_pe"], 3)
            link(TS(br_t[:, :], ps[:, 7, :], small[:, 0:1], None, ALU.mult))
            dve.tensor_copy(small[:, 8:10], small[:, 6:8]).then_inc(S["setup_dve"], 1)
            for c in range(EC):
                dve.wait_ge(S["setup_pe"], 4 + c)
                link(TT(tmp[:, 0:T], ps[:, 4 + c, :], sel_s[:, c, :].bitcast(f32), ALU.mult))
                link(dve.reduce_sum(small[:, 10 + c:11 + c], tmp[:, 0:T], AX.X))
                link(TS(tmp[:, 512 + 16 * c:528 + 16 * c], C(C_ONES, C_ONES + 16), small[:, 10 + c:11 + c], None, ALU.mult))
            dve.tensor_copy(small[:, 12:14], small[:, 6:8]).then_inc(S["setup_dve"], 1)
            dve.wait_ge(S["setup_act"], 5)
            for m in range(2):
                link(TT(wl_s[:, LO, m, :, :], lw_raw[:, m, :, :], wl_s[:, HI, m, :, :].bitcast(f32), ALU.subtract))
            dve.wait_ge(S["setup_act"], 6)
            for n, name in enumerate(("start",)):
                dve.tensor_copy(small[:, 16 + n:17 + n], small[:, 6:7]).then_inc(S[name], 1)
            setup_links = chain[0]
            count = [0]
            where = [setup_links]

            def link(ins):
                count[0] += 1
                ins.then_inc(S["dve_chain"], 1)
                dve.wait_ge(S["dve_chain"], where[0] + count[0])

            def handle(job, i, like):
                kind = job if isinstance(job, int) else job.rstrip("01")
                if kind == "U":
                    for b in PAIR[job]:
                        dve.wait_ge(S["u_hi"], 4 * i + b + 1)
                        TT(buf_b[:, LO, b, :], bank(job, like, b % 2), buf_b[:, HI, b, :].bitcast(f32),
                           ALU.subtract).then_inc(S["u_ready"], 1)
                elif kind == "Z":
                    for b in PAIR[job]:
                        dve.wait_ge(S["z_full"], 4 * i + b + 1)
                        v = bank(job, like, b % 2)
                        TT(v, v, br_t[:, :], ALU.add).then_inc(S["z_sum"], 1)
                    for b in PAIR[job]:
                        dve.wait_ge(S["z_hi"], 4 * i + b + 1)
                        dve.scalar_tensor_tensor(buf_a[:, LO, b, :], bank(job, like, b % 2), 0.0,
                                                 buf_a[:, HI, b, :].bitcast(f32),
                                                 ALU.max, ALU.subtract).then_inc(S["h1_ready"], 1)
                elif kind == "Y":
                    for b in PAIR[job]:
                        dve.wait_ge(S["z2_full"], 4 * i + b + 1)
                        v = bank(job, like, b % 2).rearrange("p (c h) -> p c h", h=D)
                        TT(v, v, b1_t[:, :].unsqueeze(1).broadcast_to([128, NC, D]), ALU.add).then_inc(S["z2_sum"], 1)
                    for b in PAIR[job]:
                        dve.wait_ge(S["z2_hi"], 4 * i + b + 1)
                        TT(buf_b[:, LO, b, :], bank(job, like, b % 2), buf_b[:, HI, b, :].bitcast(f32),
                           ALU.subtract).then_inc(S["z2_ready"], 1)
                elif kind == "H":
                    for b in PAIR[job]:
                        dve.wait_ge(S["h2_hi"], 8 * i + 2 * b + 2)
                        for r0, r1, c, q in pieces(b):
                            dve.scalar_tensor_tensor(h_t[:, LO, r0:r1, b, 0:q],
                                                     bank(job, like, b % 2)[:, c].rearrange("p (r q) -> p r q", q=q),
                                                     0.0, h_t[:, HI, r0:r1, b, 0:q].bitcast(f32),
                                                     ALU.max, ALU.subtract).then_inc(S["h2_ready"], 1)
                elif isinstance(job, int):
                    p, t, k, s = LSTM[job]
                    w = width(LSTM[job])
                    g = gates[:, s, :, 0:w]
                    c = cell[:, s, 0:w]
                    acts = GATES * i + gates_before(job)
                    dve.wait_ge(S["gate_act"], acts + 2)
                    if t == 0:
                        TT(c, g[:, GI, :], g[:, GG, :], ALU.mult).then_inc(S["cell_ready"], 1)
                    else:
                        TT(g[:, GI, :], g[:, GI, :], g[:, GG, :], ALU.mult)
                        dve.wait_ge(S["gate_act"], acts + 3)
                        link(TT(c, g[:, GF, :], c, ALU.mult))
                        TT(c, c, g[:, GI, :], ALU.add).then_inc(S["cell_ready"], 1)
                    dve.wait_ge(S["tanh_done"], NL * i + job + 1)
                    link(TT(g[:, GF, :], g[:, GO, :], g[:, GG, :], ALU.mult))
                    if t == p - 1:
                        hi, lo, h = toks(HI, LSTM[job]), toks(LO, LSTM[job]), cols(gates[:, s, GF, :], LSTM[job])
                    else:
                        hi, lo, h = rec[:, s, HI, 0:w], rec[:, s, LO, 0:w], g[:, GF, :]
                    link(dve.tensor_copy(hi, h))
                    TT(lo, h, hi.bitcast(f32), ALU.subtract).then_inc(S["h_ready"], 1)
                elif kind == "N":
                    k = int(job[1])
                    dve.wait_ge(S[f"ld_res{k}"], 16 * i + 16)
                    for b in PAIR[job]:
                        dve.wait_ge(S["n_full"], 4 * i + b + 1)
                        ins = TT(flat(res[:, b]), flat(res[:, b]), bank(job, like, b % 2), ALU.add)
                    ins.then_inc(S["n_summed"], 1)
                elif kind in ("S", "T"):
                    k = int(job[1])
                    if kind == "S":
                        dve.wait_ge(S["n_summed"], 2 * i + k + 1)
                    else:
                        dve.wait_ge(S["out_summed"], 2 * i + 2)
                    for m in range(8 * k, 8 * k + 8):
                        ins = dve.bn_stats(stats[:, m, :], res[:, m // NC, m % NC, :])
                    link(ins)
                    dve.tensor_copy(small[:, 20 + k:21 + k], stats[:, 0, 0:1])
                    for m in range(8 * k, 8 * k + 8):
                        ins = dve.bn_aggr(mv[:, m, :], stats[:, m, :])
                    link(ins)
                    TS(rstd[:, 8 * k:8 * k + 8], mv[:, 8 * k:8 * k + 8, 1], EPS, None, ALU.add).then_inc(S["var_ready"], 1)
                elif kind in ("A", "F"):
                    k = int(job[1])
                    dve.wait_ge(S["rstd_ready"], 4 * i + 2 * (kind == "F") + k + 1)
                    for m in range(8 * k, 8 * k + 8):
                        v = res[:, m // NC, m % NC, :]
                        ins = TS(v, v, mv[:, m, 0:1], rstd[:, m:m + 1], ALU.subtract, ALU.mult)
                        if kind == "A" and m % NC == NC - 1:
                            ins.then_inc(S["x1_norm"], 1)
                    if kind == "F":
                        ins.then_inc(S["out_ready"], 1)
                elif kind == "GX":
                    for b in PAIR[job]:
                        dve.wait_ge(S["gx_hi"], 4 * i + b + 1)
                        TT(buf_d[:, LO, b, :], bank(job, like, b % 2), buf_d[:, HI, b, :].bitcast(f32),
                           ALU.subtract).then_inc(S["gx_ready"], 1)
                elif kind == "Q":
                    for k in range(2):
                        dve.wait_ge(S["q_scaled"], 2 * i + k + 1)
                        TT(hn[:, k, :], hn[:, k, :], bank(job, like, k), ALU.max).then_inc(S["lrelu_ready"], 1)
                elif kind == "SC":
                    dve.wait_ge(S["sc_full"], i + 1)
                    s0, s1, s2 = (sm[:, k, :] for k in range(3))
                    link(TT(s0, bank(job, like, 0)[0:16, 0:E], log_b[:, :], ALU.add))
                    link(dve.tensor_tensor_scan(s1, seg[:, 2, :], s0, 0.0, ALU.add, ALU.max))
                    link(dve.tensor_tensor_scan(s2[:, ::-1], seg[:, 3, ::-1], s1[:, ::-1], 0.0, ALU.add, ALU.max))
                    TT(s0, s0, s2, ALU.subtract).then_inc(S["shifted"], 1)
                    dve.wait_ge(S["exp_done"], i + 1)
                    link(dve.tensor_tensor_scan(s1, seg[:, 0, :], s2, 0.0, ALU.mult, ALU.add))
                    link(dve.tensor_tensor_scan(s0[:, ::-1], seg[:, 1, ::-1], s1[:, ::-1], 0.0, ALU.mult, ALU.max))
                    link(dve.reciprocal(s0, s0))
                    TT(s0, s0, s2, ALU.mult).then_inc(S["attn_ready"], 1)
                elif kind == "AB":
                    k = int(job[2])
                    dve.wait_ge(S["ab_full"], 2 * i + k + 1)
                    dve.wait_ge(S["v_copied"], 2 * i + 2)
                    TT(hn[:, 2 + k, :], hn[:, 2 + k, :], bank(job, like, 0), ALU.mult).then_inc(S["m_ready"], 1)
                elif kind == "MW":
                    for k in range(EC):
                        dve.wait_ge(S["mw_hi"], 2 * i + k + 1)
                        TT(buf_c[:, LO, 2 + k, :], bank(job, like, k), buf_c[:, HI, 2 + k, :].bitcast(f32),
                           ALU.subtract).then_inc(S["mw_ready"], 1)
                elif kind == "O":
                    for n, c in enumerate(PAIR[job]):
                        dve.wait_ge(S["out_full"], 4 * i + c + 1)
                        ins = TT(res[:, :, c, :], res[:, :, c, :],
                                 bank(job, like, n).rearrange("p (b d) -> p b d", b=G), ALU.add)
                    ins.then_inc(S["out_summed"], 1)

            for job, g in BEFORE + body(0):
                handle(job, g, g)
            before_loop = setup_links + count[0]
            with dve.Fori(1, ITERS - 1) as i:
                count[0] = 0
                where[0] = DVE_LINKS * i + (before_loop - DVE_LINKS)
                for job, off in BODY:
                    handle(job, i + off, 1 + off)
                assert count[0] == DVE_LINKS, count[0]
            where[0], count[0] = before_loop, (ITERS - 2) * DVE_LINKS
            for job, g in body(ITERS - 1) + AFTER:
                handle(job, g, g)

        @block.tensor
        def _(pe):
            mm = pe.matmul

            def exact3(o, l, r, start, stop):
                mm(o, l[HI], r[HI], start=start, stop=False)
                mm(o, l[HI], r[LO], start=False, stop=False)
                return mm(o, l[LO], r[HI], start=False, stop=stop)

            ones = C(C_ONES, C_ONES + 128)
            pe.wait_ge(S["setup_dve"], 1)
            mm(ps[:, 0, 0:E], ones[0:1, :], tmp[0:1, 0:E], start=True, stop=True)
            mm(ps[:, 1, 0:D], ones[0:1, :], b1_t[0:1, :], start=True, stop=True).then_inc(S["setup_pe"], 1)
            pe.wait_ge(S["setup_dve"], 2)
            perm = tmp[:, 512:1024].rearrange("p (c r) -> p c r", c=EC)
            spread = tmp[:, 0:512].rearrange("p (k n) -> p k n", k=4)
            for k in range(2):
                for c in range(EC):
                    mm(ps[:, 2, k * E:(k + 1) * E], spread[:, 2 * k + c, :], perm[:, c, :], start=(c == 0), stop=(c == EC - 1))
            for rc in range(EC):
                for c in range(EC):
                    m = mm(ps[:, 3, rc:rc + 1], perm[:, c, rc * 128:(rc + 1) * 128], edge_f[:, c:c + 1], start=(c == 0), stop=(c == EC - 1))
            m.then_inc(S["setup_pe"], 1)
            pe.wait_ge(S["setup_dve"], 3)
            pe.wait_ge(S["ones_r"], 1)
            for c in range(NC):
                for hl in (HI, LO):
                    m = mm(ps[:, 7, :], ones_r, adj_s[:, hl, c, :], start=(c == 0 and hl == HI), stop=(c == NC - 1 and hl == LO))
            m.then_inc(S["setup_pe"], 1)
            pe.wait_ge(S["setup_dve"], 4)
            for ec in range(EC):
                for c in range(NC):
                    for hl in (HI, LO):
                        m = mm(ps[:, 4 + ec, :], sel_g[:, c, E + ec * 128:E + (ec + 1) * 128], adj_s[:, hl, c, :],
                               start=(c == 0 and hl == HI), stop=(c == NC - 1 and hl == LO))
                m.then_inc(S["setup_pe"], 1)
            pe.wait_ge(S["setup_dve"], 5)
            for ec in range(EC):
                m = mm(ps[0:16, 6, ec * 128:(ec + 1) * 128], tmp[:, 512 + 16 * ec:528 + 16 * ec], ident[:, :], start=True, stop=True)
            m.then_inc(S["setup_pe"], 1)

            pe.wait_ge(S["start"], 1)
            def handle(job, i, like):
                kind = job if isinstance(job, int) else job.rstrip("01")
                if job in NO_PSUM:
                    return
                holder = HELD_BY[job, like]
                if holder is not None:
                    name, per, n = READ_OUT[holder[0]]
                    pe.wait_ge(S[name], per * (i + holder[1] - like) + n)
                if kind in ("U", "H"):
                    src, ready, full = (buf_a, "x_ready", "u_full") if kind == "U" else (buf_b, "z2_ready", "h2_full")
                    for b in PAIR[job]:
                        pe.wait_ge(S[ready], 4 * i + b + 1)
                        for c in range(NC):
                            m = exact3(bank(job, like, b % 2), [src[:, hl, b, c * 128:(c + 1) * 128] for hl in (HI, LO)],
                                       [adj_s[:, hl, c, :] for hl in (HI, LO)], c == 0, c == NC - 1)
                        m.then_inc(S[full], 1)
                elif kind == "Z":
                    for b in PAIR[job]:
                        pe.wait_ge(S["u_ready"], 4 * i + b + 1)
                        exact3(bank(job, like, b % 2), [wg_s[:, hl, 0, :] for hl in (HI, LO)],
                               [buf_b[:, hl, b, :] for hl in (HI, LO)], True, True).then_inc(S["z_full"], 1)
                elif kind == "Y":
                    for b in PAIR[job]:
                        pe.wait_ge(S["h1_ready"], 4 * i + b + 1)
                        for c in range(NC):
                            m = exact3(bank(job, like, b % 2)[:, c * 128:(c + 1) * 128],
                                       [buf_a[:, hl, b, c * 128:(c + 1) * 128] for hl in (HI, LO)],
                                       [wg_s[:, hl, 1, :] for hl in (HI, LO)], True, True)
                        m.then_inc(S["z2_full"], 1)
                elif isinstance(job, int):
                    p, t, k, s = LSTM[job]
                    if job == 0:
                        pe.wait_ge(S["h2_ready"], 8 * i + 8)
                    if p > 1 and t == 0:
                        pe.wait_ge(S["h_ready"], NL * i + done_before(job))
                    wi, wh = ([[wl_s[:, hl, m, p - 1, g * D:(g + 1) * D] for hl in (HI, LO)] for g in range(4)]
                              for m in range(2))
                    todo = gates_of(LSTM[job])
                    o = {g: cols(bank(job, like, g), LSTM[job]) for g in todo}
                    for g in todo:
                        m = exact3(o[g], wi[g], [toks(hl, LSTM[job]) for hl in (HI, LO)], True, t == 0)
                        if t == 0:
                            m.then_inc(S["gate_full"], 1)
                    if t:
                        pe.wait_ge(S["h_ready"], NL * i + last_user(job) + 1)
                        for g in todo:
                            exact3(o[g], wh[g], [cols(rec[:, s, hl, :], LSTM[job]) for hl in (HI, LO)], False, True)\
                                .then_inc(S["gate_full"], 1)
                elif kind == "N":
                    pe.wait_ge(S["hn_ready"], 8 * i + 4 * int(job[1]) + 4)
                    for b in PAIR[job]:
                        for c in range(NC):
                            cc = slice(c * 128, (c + 1) * 128)
                            m = pe.transpose(bank(job, like, b % 2)[:, cc], hn[:, b, cc], ident[:, :])
                        m.then_inc(S["n_full"], 1)
                elif kind == "GX":
                    for b in PAIR[job]:
                        pe.wait_ge(S["x1_ready"], 4 * i + b + 1)
                        for c in range(NC):
                            for hl in (HI, LO):
                                m = mm(bank(job, like, b % 2), buf_c[:, hl, b, c * 128:(c + 1) * 128], sel_g[:, c, :],
                                       start=(c == 0 and hl == HI), stop=(c == NC - 1 and hl == LO))
                        m.then_inc(S["gx_full"], 1)
                elif kind in ("Q", "V"):
                    n = int(kind == "V")
                    pe.wait_ge(S["gx_ready"], 4 * i + 4)
                    for k in range(2):
                        exact3(bank(job, like, k).rearrange("p (b e) -> p b e", b=2), [wa_s[:, hl, n, :] for hl in (HI, LO)],
                               [buf_d[:, hl, 2 * k:2 * k + 2, n * E:(n + 1) * E] for hl in (HI, LO)], True, True)\
                            .then_inc(S["v_full" if n else "q_full"], 1)
                elif kind == "SC":
                    pe.wait_ge(S["lrelu_ready"], 2 * i + 2)
                    for b in range(G):
                        m = mm(bank(job, like, 0)[0:16, 0:E], a_blk[:, b, :], hn[:, b // 2, (b % 2) * E:(b % 2 + 1) * E],
                               start=(b == 0), stop=(b == G - 1))
                    m.then_inc(S["sc_full"], 1)
                elif kind == "AB":
                    k = int(job[2])
                    pe.wait_ge(S["attn_ready"], i + 1)
                    for b in range(2):
                        m = mm(bank(job, like, 0)[:, b * E:(b + 1) * E], eall[:, 2 * k + b, :], sm[:, 0, :], start=True, stop=True)
                    m.then_inc(S["ab_full"], 1)
                elif kind == "MW":
                    pe.wait_ge(S["m_split"], 2 * i + 2)
                    for ec in range(EC):
                        for b in range(G):
                            c0 = (b % 2) * E + ec * 128
                            m = exact3(bank(job, like, ec)[:, b * D:(b + 1) * D],
                                       [buf_c[:, hl, b // 2, c0:c0 + 128] for hl in (HI, LO)],
                                       [wa_s[:, hl, 2, :] for hl in (HI, LO)], True, True)
                        m.then_inc(S["mw_full"], 1)
                elif kind == "O":
                    pe.wait_ge(S["mw_ready"], 2 * i + 2)
                    for n, c in enumerate(PAIR[job]):
                        for ec in range(EC):
                            for hl in (HI, LO):
                                m = mm(bank(job, like, n), sel_s[:, ec, c * 128:(c + 1) * 128], buf_c[:, hl, 2 + ec, :],
                                       start=(ec == 0 and hl == HI), stop=(ec == EC - 1 and hl == LO))
                        m.then_inc(S["out_full"], 1)

            in_order(pe, handle)


def kernel(x, adj, L0_gnn_Wg0, L0_gnn_bg0, L0_gnn_Wg1, L0_gnn_bg1, L0_gnn_Wih, L0_gnn_Whh, L0_gnn_bih,
           L0_gnn_bhh, L1_gnn_W_lin, L1_gnn_W_val, L1_gnn_a, L1_gnn_W_out, L1_gnn_src, L1_gnn_dst):
    import numpy as np
    import concourse.bacc as bacc
    from concourse.bass_utils import run_bass_kernel_spmd

    order = np.concatenate([np.arange(r, T, R) for r in range(R)])
    place = np.argsort(order)

    consts = np.zeros((128, C_END), np.float32)
    consts[:, C_ID:C_ID + 128] = np.eye(128)
    d, col = np.arange(128)[:, None], np.arange(16)[None, :]
    for b in range(G):
        consts[:, C_MASK + 16 * b:C_MASK + 16 * b + 16] = col == HEADS * b + d // (D // HEADS)
        consts[0:16, C_EALL + 128 * b:C_EALL + 128 * b + 128] = (col == HEADS * b + d // (D // HEADS)).T
    consts[:, C_NODE:C_NODE + NC] = order.reshape(NC, 128).T
    consts[:, C_NROW:C_NROW + T] = order
    consts[:, C_IOTA:C_IOTA + E] = np.arange(E)
    consts[:, C_EDGE:C_EDGE + EC] = np.arange(E).reshape(EC, 128).T
    consts[:, C_ONES:C_ONES + 128] = 1.0

    X = np.asarray(x)[:, order, :].reshape(ITERS, G, NC, 128, D).transpose(0, 3, 1, 2, 4)
    A = np.asarray(adj)[order][:, order].T.reshape(NC, 128, T).transpose(1, 0, 2)
    src, dst = np.asarray(L1_gnn_src), np.asarray(L1_gnn_dst)
    cols = np.concatenate([src.reshape(EC, 128), dst.reshape(EC, 128)]).T
    rows = np.concatenate([src, dst])[None, :]
    stack = lambda ws: np.concatenate([np.asarray(w) for w in ws], axis=1)
    gate_cols = lambda w: np.asarray(w).transpose(2, 0, 1)
    bias = lambda v: np.asarray(v).reshape(SKIPS, 4, D).transpose(2, 0, 1)
    arrays = {
        "x": X, "adjT": A, "consts": consts, "edge_col": cols, "edge_row": rows,
        "w_gnn": stack([L0_gnn_Wg0, L0_gnn_Wg1, np.asarray(L1_gnn_W_lin).T, np.asarray(L1_gnn_W_val).T,
                        np.asarray(L1_gnn_W_out).T]),
        "b_gnn0": np.asarray(L0_gnn_bg0)[:, None], "b_gnn1": np.asarray(L0_gnn_bg1)[None, :],
        "w_ih": gate_cols(L0_gnn_Wih), "w_hh": gate_cols(L0_gnn_Whh),
        "b_ih": bias(L0_gnn_bih), "b_hh": bias(L0_gnn_bhh),
        "a_col": np.asarray(L1_gnn_a).reshape(D, 1),
    }
    arrays = {k: np.ascontiguousarray(v) for k, v in arrays.items()}
    nc = bacc.Bacc("TRN2", target_bir_lowering=False, num_devices=1)
    args = {k: nc.dram_tensor(k, v.shape, mybir.dt.from_np(v.dtype), kind="ExternalInput").ap()
            for k, v in arrays.items()}
    out = nc.dram_tensor("out", (ITERS, 128, G, NC, D), mybir.dt.float32, kind="ExternalOutput").ap()
    build(nc, out=out, **args)
    r = run_bass_kernel_spmd(nc, [arrays], core_ids=[0])
    y = r.results[0]["out"].transpose(0, 2, 3, 1, 4).reshape(B, T, D)
    return np.ascontiguousarray(y[:, place, :])
```

```python
import concourse.bass as bass
from concourse import mybir
from contextlib import ExitStack

B, T, D = 16, 512, 128
G = 4
ITERS = B // G
NC = T // 128
HEADS, E = 4, 256
EC = E // 128
SKIPS = 4
R, Q = 12, 43
RFULL = T - R * (Q - 1)
CUT = RFULL * Q
W = 2 * G * Q
W4 = 3 * (G // 2) * Q
EPS = 1e-5
LOG_EPS = 1e-8
SLOPE = 0.2
FAR = 3e38
GI, GF, GG, GO = range(4)

C_ID, C_MASK, C_NODE, C_NROW, C_IOTA, C_EDGE, C_ONES, C_EALL, C_END = (
    0, 128, 192, 196, 708, 964, 966, 1094, 1606)


def lstm_jobs():
    jobs = [(1, 0, s, s % 3) for s in range(6)]
    for p, chunks in ((2, 3), (3, 2), (4, 2)):
        jobs += [(p, t, k, k) for t in range(p) for k in range(chunks)]
    return jobs


LSTM = lstm_jobs()
NL = len(LSTM)


def width(job):
    return W4 if job[0] == 4 else W


def gates_of(job):
    return [GI, GG, GO] if job[1] == 0 else [GI, GG, GF, GO]


def done_before(n):
    p, t, k, _ = LSTM[n]
    if p == 1:
        return 0
    last = {2: (1, 0, 2 * k + 1), 3: (2, 1, k + 1), 4: (3, 2, 1)}[p]
    return 1 + next(m for m, j in enumerate(LSTM) if j[:3] == last)


def last_user(n):
    return next((m for m in range(n - 1, -1, -1) if LSTM[m][3] == LSTM[n][3]), None)


def later_before(n):
    return sum(j[1] > 0 for j in LSTM[:n])


N1 = sum(j[0] == 1 for j in LSTM)
GATES = sum(len(gates_of(j)) for j in LSTM)


def gates_before(n):
    return sum(len(gates_of(j)) for j in LSTM[:n])


PE_FIRST = """
    U0 U1 W U2 Z0 U3 Z1 Y0 Y1 H0 H1 H2 H3
"""
EW_FIRST = """
    X0 C0 C1 C2 X1 C3 X2 U0 W X3 U1 U2 Z0 U3 Z1 Y0 Y1 LW H0 H1 H2 H3
"""
PE_BODY0 = """
    0 P 1 2 U0+ 3 E U1+ 4 U2+ 5 6 7 8 9 10 11 12 L 13 Z0+ LN 14 15 16 17 Y0+ U3+ 18 19 20 21 Z1+ 22 Y1+ 23 24
    25 H0+ H1+ H2+ H3+ N0 N1 N2 N3
"""
EW_BODY0 = """
    KEYS P X0+ 0 0h 1 2 X1+ X2+ 1h 2h U0+ 3 E 3h 4 U1+ U2+ 4h 5 5h 6 7 6h 8 7h 8h 9 9h 10 10h 11 11h 12 L 13
    12h LN Z0+ 13h 14 X3+ 14h 15 15h 16 16h 17 17h Y0+ U3+ 18 18h 19 19h 20 20h 21 Z1+ 21h 22 Y1+ 22h 23 23h
    24 24h 25 25h K H0+ H1+ H2+ H3+ N0 N1 N2 N3
"""
PE_BODY = """
    0 1 2 3 U0+ U1+ 4 GX0- 5 6 7 Z0+ U2+ U3+ 8 9 GX1- Y0+ 10 Z1+ GX2- 11 GX3- 12 Q0- Q1- 13 V0- V1- SC- 14 15
    AB0- AB1- 16 Y1+ 17 MW0- MW1- 18 O0- 19 O1- 20 21 22 O2- 23 24 25 O3- H0+ H1+ H2+ H3+ N0 N1 N2 N3
"""
EW_BODY = """
    X0+ 0 1 S0- X1+ 0h 2 X2+ A0- S1- U0+ 1h 3 2h U1+ X3+ 3h 4 GX0- S2- 5 4h 6 A1- Z0+ 5h 7 U2+ 6h U3+ 8 A2-
    S3- 7h 9 A3- Y0+ GX1- 8h 9h 10 Z1+ GX2- 10h 11 GX3- 11h 12 Q0- Q1- 13 12h V0- V1- 13h SC- 14 15 14h 15h
    16 AB0- AB1- Y1+ 16h 17 17h MW0- MW1- 18 18h O0- 19 T0- O1- 19h 20 T1- 20h F0- 21 22 21h O2- 22h 23 T2-
    23h F1- F2- 24 O3- T3- 24h 25 F3- 25h K H0+ H1+ H2+ H3+ N0 N1 N2 N3
"""
PE_BODY3 = """
    0 1 2 3 4 5 GX0- 6 7 GX1- 8 9 V0- 10 11 GX2- GX3- 12 Q0- Q1- 13 14 SC- V1- 15 16 AB0- AB1- 17 MW0- MW1-
    18 19 O0- O1- 20 21 O2- 22 O3- 23 24 25 N0 N1 N2 N3 GX0 GX1 GX2 GX3 Q0 Q1 SC V0 V1 AB0 AB1 MW0 MW1 O0 O1
    O2 O3
"""
EW_BODY3 = """
    0 S0- S1- 1 0h 2 3 A0- A1- S2- 1h 2h 3h 4 GX0- 5 4h 6 5h 6h S3- 7 8 GX1- 7h 9 A2- V0- A3- 8h 10 9h 11 10h
    GX2- GX3- 11h 12 Q0- 12h 13 Q1- 13h 14 14h V1- SC- 15 16 15h AB0- AB1- 16h 17 17h MW0- MW1- 18 18h O0- 19
    T0- 19h O1- F0- 20 T1- 20h O2- 21 T2- F1- 21h 22 O3- 22h 23 T3- 23h F2- F3- 24 25 24h 25h K N0 N1 S0 S1
    N2 N3 S2 A0 A1 S3 A2 A3 GX0 GX1 GX2 GX3 Q0 Q1 SC V0 V1 AB0 AB1 MW0 MW1 O0 T0 O1 T1 O2 O3 F0 T2 T3 F1 F2
    F3
"""
ONCE = ("KEYS", "P", "E", "L", "LN")


def parse(text):
    jobs = []
    for word in text.split():
        name = word.rstrip("+-")
        jobs.append((int(name) if name.isdigit() else name, word.count("+") - word.count("-")))
    return jobs


class Order:
    def __init__(self, first, body0, body, body3):
        self.before = parse(first)
        self.body = parse(body)
        self.peeled = {0: parse(body0), ITERS - 1: parse(body3)}

    def of(self, i):
        return [(job, i + off if job not in ONCE else 0) for job, off in self.peeled.get(i, self.body)]

    def every(self):
        jobs = self.before + [j for i in range(ITERS) for j in self.of(i)]
        assert len(set(jobs)) == len(jobs)
        return jobs


PE_ORDER = Order(PE_FIRST, PE_BODY0, PE_BODY, PE_BODY3)
EW_ORDER = Order(EW_FIRST, EW_BODY0, EW_BODY, EW_BODY3)

TAKES = {"W": 2, "P": 1, "E": 2, "L": 2, "LN": 1, "SC": 1}
TAKES.update({f"{name}{k}": 2 for name in "ZY" for k in range(2)})
TAKES.update({f"{name}{k}": 1 for name in "Q V AB MW".split() for k in range(2)})
TAKES.update({f"{name}{k}": 1 for name in "U H N GX O".split() for k in range(4)})
TAKES.update({n: len(gates_of(LSTM[n])) for n in range(NL)})


def ring():
    banks, held, at, holder = {}, {}, 0, [None] * 8
    for job in PE_ORDER.every():
        banks[job] = [(at + n) % 8 for n in range(TAKES[job[0]])]
        at = (at + TAKES[job[0]]) % 8
        held[job] = list(dict.fromkeys(holder[n] for n in banks[job] if holder[n]))
        for n in banks[job]:
            holder[n] = job
    return banks, held


BANKS, HELD_BY = ring()
for _job, _off in PE_ORDER.body:
    _a, _b = (_job, 1 + _off), (_job, 2 + _off)
    assert BANKS[_a] == BANKS[_b] and HELD_BY[_b] == [(j, g + 1) for j, g in HELD_BY[_a]]

READ_OUT = {"SC": ("shifted", 1, 1)}
for _k in range(2):
    READ_OUT.update({f"Z{_k}": ("h1_ready", 4, 2 * _k + 2), f"Y{_k}": ("z2_ready", 4, 2 * _k + 2),
                     f"Q{_k}": ("lrelu_ready", 2, _k + 1), f"V{_k}": ("v_copied", 2, _k + 1),
                     f"AB{_k}": ("m_ready", 2, _k + 1), f"MW{_k}": ("mw_ready", 2, _k + 1)})
for _k in range(4):
    READ_OUT.update({f"U{_k}": ("u_ready", 4, _k + 1), f"H{_k}": ("h2_ready", 8, 2 * _k + 2),
                     f"N{_k}": ("n_summed", 4, _k + 1), f"GX{_k}": ("gx_ready", 4, _k + 1),
                     f"O{_k}": ("out_summed", 4, _k + 1)})
READ_OUT.update({n: ("gate_act", GATES, gates_before(n + 1)) for n in range(NL)})
READ_OUT.update({"W": ("bias_terms", 0, 1), "P": ("ranked", 0, 1), "E": ("selections", 0, 1), "L": ("edge_adj", 0, 1),
                 "LN": ("log_done", 0, 1)})

AHEAD = 1
WARM_START = 36
WARM = {("N0", ITERS - 1): 22, ("GX0", ITERS - 1): 26, ("AB0", ITERS - 1): 20, ("MW0", ITERS - 1): 8}
DVE_LINKS = 61


def build(nc, x, adjT, consts, edge_col, edge_row, w_gnn, b_gnn0, b_gnn1, w_ih, w_hh, b_ih, b_hh,
          a_col, out):
    f32, f32r, i32 = mybir.dt.float32, mybir.dt.float32r, mybir.dt.int32
    ALU, ACT, AX = mybir.AluOpType, mybir.ActivationFunctionType, mybir.AxisListType
    HI, LO = 0, 1

    ctx = ExitStack()
    with ctx:
        def sb(name, shape, dt=f32):
            return ctx.enter_context(nc.sbuf_tensor(name, shape, dt))

        def sem(name):
            return ctx.enter_context(nc.semaphore(name))

        adj_s = sb("adj_s", [128, 2, NC, T], f32r)
        wg_s = sb("wg_s", [128, 2, 2, D], f32r)
        wa_s = sb("wa_s", [128, 2, 3, D], f32r)
        wl_s = sb("wl_s", [128, 2, 2, SKIPS, 4 * D], f32r)
        sel_g = sb("sel_g", [128, NC, 2 * E], f32r)
        sel_s = sb("sel_s", [128, EC, T], f32r)
        br_t = sb("br_t", [128, T])
        b1_t = sb("b1_t", [128, D])
        lbias = sb("lbias", [128, 2, SKIPS, 4])
        ident = sb("ident", [128, 128])
        eall = sb("eall", [16, G, 128])
        a_blk = sb("a_blk", [128, G, 16])
        log_b = sb("log_b", [16, E])
        seg = sb("seg", [16, 4, E])
        half_c = sb("half_c", [128, 1])
        eps8 = sb("eps8", [128, 1])

        x_in = sb("x_in", [128, 2, NC, D])
        buf_a = sb("buf_a", [128, 2, G, T], f32r)
        buf_b = sb("buf_b", [128, 2, G, T], f32r)
        h_t = sb("h_t", [128, 2, R, G, Q], f32r)
        gates = sb("gates", [128, 3, 4, W])
        cell = sb("cell", [128, 3, W])
        rec = sb("rec", [128, 3, 2, W], f32r)
        hn = sb("hn", [128, G, T])
        res = sb("res", [128, G, NC, D])
        buf_c = sb("buf_c", [128, 2, G, T], f32r)
        buf_d = sb("buf_d", [128, 2, G, T], f32r)
        stats = sb("stats", [128, G, NC, 6])
        mv = sb("mv", [128, G, NC, 2])
        rstd = sb("rstd", [128, G, NC])
        sm = sb("sm", [16, 3, E])

        ps = ctx.enter_context(nc.psum_tensor("ps", [128, 8, 512], f32))

        names = ("ld_x0 ld_x1 ld_res0 ld_res1 ld_adj0 ld_adj1 ld_adj2 ld_adj3 ld_const ld_edge ld_ident ld_w "
                 "ld_lw ld_b st_out "
                 "cleared adj_hi adj_split w_hi w_split lw_hi lw_split0 lw_split1 row_sums bias_terms keyed "
                 "keys_spread ranked sorted selections dst_rows edge_adj edge_rows log_done "
                 "x_hi x_ready u_full u_hi u_ready z_full z_sum z_hi h1_ready z2_full z2_sum z2_hi z2_ready "
                 "h2_full h2_hi h2_ready gate_full gate_act cell1_ready added_ready cell_ready tanh_done h_hi h_ready "
                 "hn_ready0 hn_ready1 n_full var_ready rstd_ready x1_norm x1_hi x1_ready gx_full gx_hi gx_ready "
                 "q_full q_scaled v_full v_copied lrelu_ready sc_full shifted exp_done attn_ready ab_full "
                 "m_ready m_hi m_split mw_full mw_hi mw_ready out_full out_ready "
                 "n_summed out_summed ones_r dve_chain").split()
        S = {n: sem(n) for n in names}

        block = ctx.enter_context(nc.Block())

        def need(eng, name, value):
            if not isinstance(value, int) or value > 0:
                eng.wait_ge(S[name], value)

        def in_order(eng, order, handle):
            for job, g in order.before + order.of(0):
                handle(job, g, g)
            with eng.Fori(1, ITERS - 1) as i:
                for job, off in order.body:
                    handle(job, i + off, 1 + off)
            for job, g in order.of(ITERS - 1):
                handle(job, g, g)

        def bank(job, like, n):
            return ps[:, BANKS[job, like][n], :]

        def norm_part(ap, job):
            k = int(job[1])
            return ap[:, k] if job[0] in "SA" else ap[:, :, k]

        def to_node_order(eng, k):
            for b in (2 * k, 2 * k + 1):
                for r0, r1, c, q in pieces(b):
                    hi, lo = (h_t[:, hl, r0:r1, b, 0:q].bitcast(f32) for hl in (HI, LO))
                    eng.tensor_tensor(hn[:, b, c].rearrange("p (r q) -> p r q", q=q), hi, lo, ALU.add)\
                        .then_inc(S[f"hn_ready{k}"], 1)

        def gate_bank(job, like, g):
            return bank(job, like, gates_of(LSTM[job]).index(g))

        def flat(ap):
            return ap.rearrange("p c d -> p (c d)")

        PAIR = {f"{name}{k}": (2 * k, 2 * k + 1) for name in "ZY" for k in range(2)}

        def toks(hl, job, step=None):
            p, t, k, _ = job
            t = t if step is None else step
            if p == 1:
                return h_t[:, hl, 2 * k:2 * k + 2, :, :].rearrange("p r b q -> p r (b q)")
            if p == 2:
                return h_t[:, hl, 4 * k + t:4 * k + t + 3:2, :, :].rearrange("p r b q -> p r (b q)")
            if p == 3:
                return h_t[:, hl, 6 * k + t:6 * k + t + 4:3, :, :].rearrange("p r b q -> p r (b q)")
            h = G // 2
            return h_t[:, hl, t:t + 9:4, h * k:h * k + h, :].rearrange("p r b q -> p r (b q)")

        def cols(ap, job):
            n = 3 if job[0] == 4 else 2
            return ap[:, 0:width(job)].rearrange("p (r c) -> p r c", r=n)

        def pieces(b):
            for r0, r1, c0, c1, q in ((0, RFULL, 0, CUT, Q), (RFULL, R, CUT, T, Q - 1)):
                yield r0, r1, slice(c0, c1), q

        w_raw = hn[:, :, :].rearrange("p b t -> p (b t)")[:, 0:5 * D]
        edgerow_i = hn[:, :, :].rearrange("p b t -> p (b t)")[0:1, 1024:1024 + E].bitcast(i32)
        edge_i = hn[:, :, :].rearrange("p b t -> p (b t)")[:, 1536:1540].bitcast(i32)
        raw_adj = res[:, :, :, :].rearrange("p c t d -> p c (t d)")
        lw_raw = gates[:, :, :, :].rearrange("p a b c -> p (a b c)")[:, 0:4096]\
            .rearrange("p (a s n) -> p a s n", a=2, s=SKIPS)
        once = res[:, :, :, :].rearrange("p b c d -> p (b c d)")
        const_t, tmp = once[:, 0:C_EALL - C_NODE], once[:, 1024:2048]
        perm = tmp[:, 512:1024].rearrange("p (c r) -> p c r", c=EC)
        spread = tmp[:, 0:512].rearrange("p (k n) -> p k n", k=4)
        spread_adj = perm

        def C(a, b):
            return const_t[:, a - C_NODE:b - C_NODE]

        ones1 = cell[0:1, 0, 0:128]
        edge_f = sb("edge_f", [128, 4])
        small = sb("small", [128, 24])
        ones_r = rec[:, 0, HI, 0:128]

        @block.sync
        def _(sp):
            def load_x(it, batches):
                for b in batches:
                    if G * it + b >= 2:
                        sp.wait_ge(S["x_ready"], G * it + b - 1)
                    sp.dma_start(x_in[:, b % 2, :, :], x[it, :, b]).then_inc(S[f"ld_x{b % 2}"], 16)

            def store(it):
                for c in range(NC):
                    sp.wait_ge(S["out_ready"], 4 * it + c + 1)
                    sp.dma_start(out[it, :, c], res[:, :, c, :]).then_inc(S["st_out"], 16)

            def load_adj(c):
                sp.dma_start(raw_adj[:, c, :], adjT[:, c]).then_inc(S[f"ld_adj{c}"], 16)

            load_adj(0)
            load_x(0, [0])
            for c in range(1, NC):
                load_adj(c)
            load_x(0, [1])
            sp.dma_start(w_raw, w_gnn).then_inc(S["ld_w"], 16)
            sp.dma_start(b1_t[0:1, :], b_gnn1).then_inc(S["ld_b"], 16)
            sp.dma_start(small[:, 0:1], b_gnn0).then_inc(S["ld_b"], 16)
            sp.dma_start(small[:, 1:2], a_col).then_inc(S["ld_b"], 16)
            sp.dma_start(lbias[:, 0, :, :], b_ih).then_inc(S["ld_b"], 16)
            sp.dma_start(lbias[:, 1, :, :], b_hh).then_inc(S["ld_b"], 16)
            sp.dma_start(a_blk[:, :, :].rearrange("p b h -> p (b h)"),
                         consts[:, C_MASK:C_MASK + 64]).then_inc(S["ld_b"], 16)
            load_x(0, [2, 3])
            sp.dma_start(lw_raw[:, 0, :, :], w_ih).then_inc(S["ld_lw"], 16)
            sp.dma_start(lw_raw[:, 1, :, :], w_hh).then_inc(S["ld_lw"], 16)
            sp.dma_start(ident[:, :], consts[:, C_ID:C_ID + 128]).then_inc(S["ld_ident"], 16)
            sp.dma_start(eall[:, :, :].rearrange("p b h -> p (b h)"),
                         consts[0:16, C_EALL:C_EALL + 512]).then_inc(S["ld_ident"], 16)
            sp.dma_start(edge_i, edge_col).then_inc(S["ld_edge"], 16)
            sp.dma_start(edgerow_i, edge_row).then_inc(S["ld_edge"], 16)
            sp.wait_ge(S["adj_split"], NC)
            sp.dma_start(const_t, consts[:, C_NODE:C_EALL]).then_inc(S["ld_const"], 16)
            for it in range(ITERS):
                if it + 1 < ITERS:
                    load_x(it + 1, range(G))
                if it == 0:
                    sp.wait_ge(S["log_done"], 1)
                else:
                    store(it - 1)
                    sp.wait_ge(S["st_out"], 16 * NC * it)
                for k in range(2):
                    pair = slice(2 * k, 2 * k + 2)
                    sp.dma_start(res[:, pair, :, :], x[it, :, pair]).then_inc(S[f"ld_res{k}"], 16)
            store(ITERS - 1)
            sp.wait_ge(S["st_out"], 16 * NC * ITERS)

        @block.gpsimd
        def _(pool):
            pool.memset(ones_r.bitcast(f32), 1.0).then_inc(S["ones_r"], 1)
            pool.memset(ones1, 1.0).then_inc(S["ones_r"], 1)
            pool.memset(h_t[:, :, :, :, :].bitcast(f32), 0.0).then_inc(S["cleared"], 1)
            pool.memset(half_c[:, :], -0.5).then_inc(S["cleared"], 1)
            pool.memset(eps8[:, :], LOG_EPS).then_inc(S["cleared"], 1)
            pool.memset(seg[:, :, :], 0.0).then_inc(S["cleared"], 1)

            def handle(job, i, like):
                kind = str(job).rstrip("0123")
                if isinstance(job, int):
                    p, t, _, s = LSTM[job]
                    w = width(LSTM[job])
                    g, c = gates[:, s, :, 0:w], cell[:, s, 0:w]
                    if p == 1:
                        pool.wait_ge(S["gate_act"], GATES * i + gates_before(job) + 2)
                        pool.tensor_tensor(c, g[:, GI, :], g[:, GG, :], ALU.mult).then_inc(S["cell1_ready"], 1)
                    elif t:
                        pool.wait_ge(S["gate_act"], GATES * i + gates_before(job) + 2)
                        pool.tensor_tensor(g[:, GI, :], g[:, GI, :], g[:, GG, :], ALU.mult)\
                            .then_inc(S["added_ready"], 1)
                elif kind == "X":
                    b = int(job[1])
                    pool.wait_ge(S["x_hi"], 4 * i + b + 1)
                    pool.tensor_tensor(buf_a[:, LO, b, :], flat(x_in[:, b % 2]), buf_a[:, HI, b, :].bitcast(f32),
                                       ALU.subtract).then_inc(S["x_ready"], 1)
                elif job == "K":
                    pool.wait_ge(S["h_ready"], NL * i + NL)
                    need(pool, "m_split", 2 * i)
                    to_node_order(pool, 1)
                elif job == "LW":
                    pool.wait_ge(S["lw_hi"], 2)
                    pool.tensor_tensor(wl_s[:, LO, 1, :, :], lw_raw[:, 1, :, :], wl_s[:, HI, 1, :, :].bitcast(f32),
                                       ALU.subtract).then_inc(S["lw_split1"], 1)
                elif kind in ("S", "T"):
                    k = int(job[1])
                    pool.wait_ge(S["var_ready"], 8 * i + 4 * (job[0] == "T") + k + 1)
                    r = norm_part(rstd, job)
                    pool.tensor_tensor(r, r, half_c[:, 0:1].broadcast_to([128, 4]), ALU.pow)\
                        .then_inc(S["rstd_ready"], 1)
                elif like == ITERS - 1 and kind in ("A", "AB"):
                    pass
                elif kind == "A":
                    b = int(job[1])
                    pool.wait_ge(S["x1_hi"], 4 * i + b + 1)
                    pool.tensor_tensor(buf_c[:, LO, b, :], flat(res[:, b]), buf_c[:, HI, b, :].bitcast(f32),
                                       ALU.subtract).then_inc(S["x1_ready"], 1)
                elif kind == "AB":
                    k = int(job[2])
                    pool.wait_ge(S["m_hi"], 2 * i + k + 1)
                    pool.tensor_tensor(buf_c[:, LO, k, :], hn[:, 2 + k, :], buf_c[:, HI, k, :].bitcast(f32),
                                       ALU.subtract).then_inc(S["m_split"], 1)

            in_order(pool, EW_ORDER, handle)

        @block.scalar
        def _(act):
            def handle(job, i, like):
                kind = job if isinstance(job, int) else job.rstrip("0123")
                if kind == "C":
                    c = int(job[1])
                    act.wait_ge(S[f"ld_adj{c}"], 16)
                    act.activation(adj_s[:, HI, c, :], raw_adj[:, c, :], ACT.Copy).then_inc(S["adj_hi"], 1)
                elif kind == "W":
                    act.wait_ge(S["ld_w"], 16)
                    act.activation(flat(wg_s[:, HI]), w_raw[:, 0:2 * D], ACT.Copy).then_inc(S["w_hi"], 1)
                    act.activation(flat(wa_s[:, HI]), w_raw[:, 2 * D:5 * D], ACT.Copy).then_inc(S["w_hi"], 1)
                elif kind == "LW":
                    act.wait_ge(S["ld_lw"], 32)
                    for m in range(2):
                        act.activation(wl_s[:, HI, m, :, :], lw_raw[:, m, :, :], ACT.Copy).then_inc(S["lw_hi"], 1)
                elif kind == "LN":
                    act.wait_ge(S["edge_rows"], 1)
                    act.activation(log_b[:, :], bank(job, like, 0)[0:16, 0:E], ACT.Ln, bias=eps8[0:16, :])\
                        .then_inc(S["log_done"], 1)
                elif kind == "X":
                    b = int(job[-1])
                    act.wait_ge(S[f"ld_x{b % 2}"], 32 * i + 16 * (b // 2) + 16)
                    need(act, "z2_full", 4 * i)
                    act.activation(buf_a[:, HI, b, :], flat(x_in[:, b % 2]), ACT.Copy).then_inc(S["x_hi"], 1)
                elif kind == "U":
                    b = int(job[-1])
                    act.wait_ge(S["u_full"], 4 * i + b + 1)
                    act.activation(buf_b[:, HI, b, :], bank(job, like, 0), ACT.Copy).then_inc(S["u_hi"], 1)
                elif kind == "Z":
                    for b in PAIR[job]:
                        act.wait_ge(S["z_sum"], 4 * i + b + 1)
                        act.activation(buf_a[:, HI, b, :], bank(job, like, b % 2), ACT.Relu).then_inc(S["z_hi"], 1)
                elif kind == "Y":
                    for b in PAIR[job]:
                        act.wait_ge(S["z2_sum"], 4 * i + b + 1)
                        act.activation(buf_b[:, HI, b, :], bank(job, like, b % 2), ACT.Copy).then_inc(S["z2_hi"], 1)
                elif kind == "H":
                    b = int(job[-1])
                    need(act, f"hn_ready{b // 2}", 4 * i + 2 * (b % 2) - 2)
                    act.wait_ge(S["h2_full"], 4 * i + b + 1)
                    for r0, r1, c, q in pieces(b):
                        act.activation(h_t[:, HI, r0:r1, b, 0:q],
                                       bank(job, like, 0)[:, c].rearrange("p (r q) -> p r q", q=q),
                                       ACT.Relu).then_inc(S["h2_hi"], 1)
                elif isinstance(job, int):
                    p, _, _, s = LSTM[job]
                    w = width(LSTM[job])
                    before = last_user(job)
                    for n, g in enumerate(gates_of(LSTM[job])):
                        act.wait_ge(S["gate_full"], GATES * i + gates_before(job) + n + 1)
                        if n == 0 and before is not None:
                            act.wait_ge(S["h_ready"], NL * i + before + 1)
                        act.activation(gates[:, s, g, 0:w], gate_bank(job, like, g)[:, 0:w],
                                       ACT.Tanh if g == GG else ACT.Sigmoid,
                                       bias=lbias[:, 0, p - 1, g:g + 1]).then_inc(S["gate_act"], 1)
                elif kind[-1] == "h":
                    job = int(kind[:-1])
                    s, w = LSTM[job][3], width(LSTM[job])
                    if LSTM[job][0] == 1:
                        act.wait_ge(S["cell1_ready"], N1 * i + job + 1)
                    else:
                        act.wait_ge(S["cell_ready"], (NL - N1) * i + job - N1 + 1)
                    act.activation(gates[:, s, GG, 0:w], cell[:, s, 0:w], ACT.Tanh).then_inc(S["tanh_done"], 1)
                elif kind == "A":
                    b = int(job[1])
                    act.wait_ge(S["x1_norm"], 4 * i + b + 1)
                    act.activation(buf_c[:, HI, b, :], flat(res[:, b]), ACT.Copy).then_inc(S["x1_hi"], 1)
                elif kind == "GX":
                    b = int(job[-1])
                    act.wait_ge(S["gx_full"], 4 * i + b + 1)
                    act.activation(buf_d[:, HI, b, :], bank(job, like, 0), ACT.Copy).then_inc(S["gx_hi"], 1)
                elif kind == "Q":
                    k = int(job[-1])
                    act.wait_ge(S["q_full"], 2 * i + k + 1)
                    act.activation(hn[:, k, :], bank(job, like, 0), ACT.Copy, scale=SLOPE).then_inc(S["q_scaled"], 1)
                elif kind == "V":
                    k = int(job[-1])
                    act.wait_ge(S["v_full"], 2 * i + k + 1)
                    act.activation(hn[:, 2 + k, :], bank(job, like, 0), ACT.Copy).then_inc(S["v_copied"], 1)
                elif kind == "SC":
                    act.wait_ge(S["shifted"], i + 1)
                    act.activation(sm[:, 2, :], sm[:, 0, :], ACT.Exp).then_inc(S["exp_done"], 1)
                elif kind == "AB":
                    k = int(job[2])
                    act.wait_ge(S["m_ready"], 2 * i + k + 1)
                    act.activation(buf_c[:, HI, k, :], hn[:, 2 + k, :], ACT.Copy).then_inc(S["m_hi"], 1)
                elif kind == "MW":
                    k = int(job[-1])
                    act.wait_ge(S["mw_full"], 2 * i + k + 1)
                    act.activation(buf_c[:, HI, 2 + k, :], bank(job, like, 0), ACT.Copy).then_inc(S["mw_hi"], 1)

            in_order(act, EW_ORDER, handle)

        @block.vector
        def _(dve):
            TT, TS = dve.tensor_tensor, dve.tensor_scalar
            count = [0]
            where = [0]

            def link(ins):
                count[0] += 1
                ins.then_inc(S["dve_chain"], 1)
                dve.wait_ge(S["dve_chain"], where[0] + count[0])

            def bias_terms(job):
                dve.wait_ge(S["w_hi"], 2)
                TT(flat(wg_s[:, LO]), w_raw[:, 0:2 * D], flat(wg_s[:, HI]).bitcast(f32), ALU.subtract)\
                    .then_inc(S["w_split"], 1)
                TT(flat(wa_s[:, LO]), w_raw[:, 2 * D:5 * D], flat(wa_s[:, HI]).bitcast(f32), ALU.subtract)
                dve.wait_ge(S["ld_b"], 96)
                link(TT(lbias[:, 0, :, :], lbias[:, 0, :, :], lbias[:, 1, :, :], ALU.add))
                link(TS(a_blk[:, :, :], a_blk[:, :, :], small[:, 1:2], None, ALU.mult))
                dve.wait_ge(S["row_sums"], 1)
                TS(br_t[:, :], bank(job, 0, 0), small[:, 0:1], None, ALU.mult)
                link(dve.tensor_copy(b1_t[:, :], bank(job, 0, 1)[:, 0:D]))
                dve.tensor_copy(small[:, 16:17], small[:, 1:2]).then_inc(S["bias_terms"], 1)

            row = tmp[0:1, 0:E]
            key = small[:, 2:4]

            def edge_keys():
                dve.wait_ge(S["ld_edge"], 32)
                dve.wait_ge(S["ld_const"], 16)
                dve.tensor_copy(edge_f[:, :], edge_i)
                link(dve.tensor_copy(row, edgerow_i))
                for c in range(EC):
                    link(TS(key[:, c:c + 1], edge_f[:, c:c + 1], float(E), None, ALU.mult))
                    link(TT(key[:, c:c + 1], key[:, c:c + 1], C(C_EDGE + c, C_EDGE + c + 1), ALU.add))
                link(TS(row, row, float(E), None, ALU.mult))
                TT(row, row, C(C_IOTA, C_IOTA + E)[0:1, :], ALU.add).then_inc(S["keyed"], 1)

            def edge_ranks(job):
                dve.wait_ge(S["keys_spread"], 1)
                rank = small[:, 4:6]
                for c in range(EC):
                    link(TS(tmp[:, 0:E], bank(job, 0, 0)[:, 0:E], key[:, c:c + 1], None, ALU.is_lt))
                    link(dve.reduce_sum(rank[:, c:c + 1], tmp[:, 0:E], AX.X))
                    link(TS(perm[:, c, :], C(C_IOTA, C_IOTA + E), rank[:, c:c + 1], None, ALU.is_equal))
                for k in range(4):
                    link(TS(spread[:, k, :], C(C_ONES, C_ONES + 128), edge_f[:, k:k + 1], None, ALU.mult))
                dve.tensor_copy(small[:, 17:18], small[:, 1:2]).then_inc(S["ranked"], 1)

            def edge_selections(job):
                dve.wait_ge(S["sorted"], 1)
                both = bank(job, 0, 0)
                for c in range(NC):
                    node = C(C_NODE + c, C_NODE + c + 1)
                    link(TS(sel_g[:, c, E:2 * E], both[:, E:2 * E], node, None, ALU.is_equal))
                    dve.scalar_tensor_tensor(sel_g[:, c, 0:E], both[:, 0:E], node,
                                             sel_g[:, c, E:2 * E].bitcast(f32), ALU.is_equal, ALU.add)
                link(dve.tensor_copy(small[:, 6:8], bank(job, 0, 1)[:, 0:EC]))
                for c in range(EC):
                    TS(sel_s[:, c, :], C(C_NROW, C_NROW + T), small[:, 6 + c:7 + c], None, ALU.is_equal)
                link(dve.tensor_copy(sm[:, 0, :], both[0:16, 0:E]))
                dve.wait_ge(S["cleared"], 4)
                link(TT(seg[:, 0, 1:E], sm[:, 0, 1:E], sm[:, 0, 0:E - 1], ALU.is_equal))
                link(TT(seg[:, 1, 0:E - 1], sm[:, 0, 1:E], sm[:, 0, 0:E - 1], ALU.is_equal))
                for k in range(2):
                    link(TS(seg[:, 2 + k, :], seg[:, k, :], FAR, -FAR, ALU.mult, ALU.add))
                dve.tensor_copy(small[:, 18:19], small[:, 1:2]).then_inc(S["selections"], 1)

            def edge_adj(job):
                for c in range(EC):
                    dve.wait_ge(S["dst_rows"], 1 + c)
                    link(TT(tmp[:, 0:T], bank(job, 0, c), sel_s[:, c, :].bitcast(f32), ALU.mult))
                    link(dve.reduce_sum(small[:, 10 + c:11 + c], tmp[:, 0:T], AX.X))
                    link(TS(spread_adj[:, c, 0:16], C(C_ONES, C_ONES + 16), small[:, 10 + c:11 + c], None, ALU.mult))
                dve.tensor_copy(small[:, 19:20], small[:, 1:2]).then_inc(S["edge_adj"], 1)

            def handle(job, i, like):
                kind = job if isinstance(job, int) else job.rstrip("0123")
                if isinstance(job, int):
                    new_cell(job, i)
                elif kind[-1] == "h":
                    new_state(int(kind[:-1]), i)
                elif kind == "C":
                    c = int(job[1])
                    dve.wait_ge(S["adj_hi"], c + 1)
                    TT(adj_s[:, LO, c, :], raw_adj[:, c, :], adj_s[:, HI, c, :].bitcast(f32), ALU.subtract)\
                        .then_inc(S["adj_split"], 1)
                elif kind == "W":
                    bias_terms(job)
                elif kind == "KEYS":
                    edge_keys()
                elif kind == "LW":
                    dve.wait_ge(S["lw_hi"], 1)
                    TT(wl_s[:, LO, 0, :, :], lw_raw[:, 0, :, :], wl_s[:, HI, 0, :, :].bitcast(f32),
                       ALU.subtract).then_inc(S["lw_split0"], 1)
                elif kind == "P":
                    edge_ranks(job)
                elif kind == "E":
                    edge_selections(job)
                elif kind == "L":
                    edge_adj(job)
                elif kind == "U":
                    b = int(job[-1])
                    dve.wait_ge(S["u_hi"], 4 * i + b + 1)
                    TT(buf_b[:, LO, b, :], bank(job, like, 0), buf_b[:, HI, b, :].bitcast(f32),
                       ALU.subtract).then_inc(S["u_ready"], 1)
                elif kind == "Z":
                    for b in PAIR[job]:
                        dve.wait_ge(S["z_full"], 4 * i + b + 1)
                        v = bank(job, like, b % 2)
                        TT(v, v, br_t[:, :], ALU.add).then_inc(S["z_sum"], 1)
                    for b in PAIR[job]:
                        dve.wait_ge(S["z_hi"], 4 * i + b + 1)
                        dve.scalar_tensor_tensor(buf_a[:, LO, b, :], bank(job, like, b % 2), 0.0,
                                                 buf_a[:, HI, b, :].bitcast(f32),
                                                 ALU.max, ALU.subtract).then_inc(S["h1_ready"], 1)
                elif kind == "Y":
                    for b in PAIR[job]:
                        dve.wait_ge(S["z2_full"], 4 * i + b + 1)
                        v = bank(job, like, b % 2).rearrange("p (c h) -> p c h", h=D)
                        TT(v, v, b1_t[:, :].unsqueeze(1).broadcast_to([128, NC, D]), ALU.add).then_inc(S["z2_sum"], 1)
                    for b in PAIR[job]:
                        dve.wait_ge(S["z2_hi"], 4 * i + b + 1)
                        TT(buf_b[:, LO, b, :], bank(job, like, b % 2), buf_b[:, HI, b, :].bitcast(f32),
                           ALU.subtract).then_inc(S["z2_ready"], 1)
                elif kind == "H":
                    b = int(job[-1])
                    dve.wait_ge(S["h2_hi"], 8 * i + 2 * b + 2)
                    for r0, r1, c, q in pieces(b):
                        dve.scalar_tensor_tensor(h_t[:, LO, r0:r1, b, 0:q],
                                                 bank(job, like, 0)[:, c].rearrange("p (r q) -> p r q", q=q),
                                                 0.0, h_t[:, HI, r0:r1, b, 0:q].bitcast(f32),
                                                 ALU.max, ALU.subtract).then_inc(S["h2_ready"], 1)
                elif kind == "K":
                    dve.wait_ge(S["h_ready"], NL * i + NL)
                    need(dve, "m_split", 2 * i)
                    to_node_order(dve, 0)
                elif kind == "N":
                    b = int(job[1])
                    dve.wait_ge(S[f"ld_res{b // 2}"], 16 * i + 16)
                    dve.wait_ge(S["n_full"], 4 * i + b + 1)
                    ins = TT(flat(res[:, b]), flat(res[:, b]), bank(job, like, 0), ALU.add)
                    ins.then_inc(S["n_summed"], 1)
                elif kind in ("S", "T"):
                    k = int(job[1])
                    dve.wait_ge(S["n_summed" if kind == "S" else "out_summed"], 4 * i + k + 1)
                    r, st, m = (norm_part(ap, job) for ap in (res, stats, mv))
                    for n in range(4):
                        ins = dve.bn_stats(st[:, n, :], r[:, n, :])
                    link(ins)
                    dve.tensor_copy(small[:, 20 + k:21 + k], small[:, 1:2])
                    for n in range(4):
                        ins = dve.bn_aggr(m[:, n, :], st[:, n, :])
                    link(ins)
                    TS(norm_part(rstd, job), m[:, :, 1], EPS, None, ALU.add).then_inc(S["var_ready"], 1)
                elif kind in ("A", "F"):
                    k = int(job[1])
                    dve.wait_ge(S["rstd_ready"], 8 * i + 4 * (kind == "F") + k + 1)
                    r, m, d = (norm_part(ap, job) for ap in (res, mv, rstd))
                    for n in range(4):
                        ins = TS(r[:, n, :], r[:, n, :], m[:, n, 0:1], d[:, n:n + 1], ALU.subtract, ALU.mult)
                    ins.then_inc(S["x1_norm" if kind == "A" else "out_ready"], 1)
                    if kind == "A" and like == ITERS - 1:
                        dve.wait_ge(S["x1_hi"], 4 * i + k + 1)
                        TT(buf_c[:, LO, k, :], flat(res[:, k]), buf_c[:, HI, k, :].bitcast(f32),
                           ALU.subtract).then_inc(S["x1_ready"], 1)
                elif kind == "GX":
                    b = int(job[-1])
                    dve.wait_ge(S["gx_hi"], 4 * i + b + 1)
                    TT(buf_d[:, LO, b, :], bank(job, like, 0), buf_d[:, HI, b, :].bitcast(f32),
                       ALU.subtract).then_inc(S["gx_ready"], 1)
                elif kind == "Q":
                    k = int(job[-1])
                    dve.wait_ge(S["q_scaled"], 2 * i + k + 1)
                    TT(hn[:, k, :], hn[:, k, :], bank(job, like, 0), ALU.max).then_inc(S["lrelu_ready"], 1)
                elif kind == "SC":
                    dve.wait_ge(S["sc_full"], i + 1)
                    s0, s1, s2 = (sm[:, k, :] for k in range(3))
                    link(TT(s0, bank(job, like, 0)[0:16, 0:E], log_b[:, :], ALU.add))
                    link(dve.tensor_tensor_scan(s1, seg[:, 2, :], s0, 0.0, ALU.add, ALU.max))
                    link(dve.tensor_tensor_scan(s2[:, ::-1], seg[:, 3, ::-1], s1[:, ::-1], 0.0, ALU.add, ALU.max))
                    TT(s0, s0, s2, ALU.subtract).then_inc(S["shifted"], 1)
                    dve.wait_ge(S["exp_done"], i + 1)
                    link(dve.tensor_tensor_scan(s1, seg[:, 0, :], s2, 0.0, ALU.mult, ALU.add))
                    link(dve.tensor_tensor_scan(s0[:, ::-1], seg[:, 1, ::-1], s1[:, ::-1], 0.0, ALU.mult, ALU.max))
                    link(dve.reciprocal(s0, s0))
                    TT(s0, s0, s2, ALU.mult).then_inc(S["attn_ready"], 1)
                elif kind == "AB":
                    k = int(job[2])
                    dve.wait_ge(S["ab_full"], 2 * i + k + 1)
                    dve.wait_ge(S["v_copied"], 2 * i + 2)
                    TT(hn[:, 2 + k, :], hn[:, 2 + k, :], bank(job, like, 0), ALU.mult).then_inc(S["m_ready"], 1)
                    if like == ITERS - 1:
                        dve.wait_ge(S["m_hi"], 2 * i + k + 1)
                        TT(buf_c[:, LO, k, :], hn[:, 2 + k, :], buf_c[:, HI, k, :].bitcast(f32),
                           ALU.subtract).then_inc(S["m_split"], 1)
                elif kind == "MW":
                    k = int(job[-1])
                    dve.wait_ge(S["mw_hi"], 2 * i + k + 1)
                    TT(buf_c[:, LO, 2 + k, :], bank(job, like, 0), buf_c[:, HI, 2 + k, :].bitcast(f32),
                       ALU.subtract).then_inc(S["mw_ready"], 1)
                elif kind == "O":
                    c = int(job[1])
                    dve.wait_ge(S["out_full"], 4 * i + c + 1)
                    ins = TT(res[:, :, c, :], res[:, :, c, :],
                             bank(job, like, 0).rearrange("p (b d) -> p b d", b=G), ALU.add)
                    ins.then_inc(S["out_summed"], 1)

            def new_cell(job, i):
                p, t, _, s = LSTM[job]
                w = width(LSTM[job])
                g, c = gates[:, s, :, 0:w], cell[:, s, 0:w]
                acts = GATES * i + gates_before(job)
                if p == 1:
                    pass
                elif t == 0:
                    dve.wait_ge(S["gate_act"], acts + 2)
                    TT(c, g[:, GI, :], g[:, GG, :], ALU.mult).then_inc(S["cell_ready"], 1)
                else:
                    dve.wait_ge(S["gate_act"], acts + 3)
                    link(TT(c, g[:, GF, :], c, ALU.mult))
                    dve.wait_ge(S["added_ready"], later_before(NL) * i + later_before(job) + 1)
                    TT(c, c, g[:, GI, :], ALU.add).then_inc(S["cell_ready"], 1)

            def new_state(job, i):
                p, t, _, s = LSTM[job]
                dve.wait_ge(S["tanh_done"], NL * i + job + 1)
                if t == p - 1:
                    hi, lo = (toks(hl, LSTM[job]) for hl in (HI, LO))
                else:
                    hi, lo = (cols(rec[:, s, hl, :], LSTM[job]) for hl in (HI, LO))
                h, o, tanh_c = (cols(gates[:, s, n, :], LSTM[job]) for n in (GF, GO, GG))
                link(TT(h, o, tanh_c, ALU.mult))
                dve.tensor_copy(hi, h).then_inc(S["h_hi"], 1)
                dve.wait_ge(S["h_hi"], NL * i + job + 1)
                TT(lo, h, hi.bitcast(f32), ALU.subtract).then_inc(S["h_ready"], 1)

            for job, g in EW_ORDER.before + EW_ORDER.of(0):
                handle(job, g, g)
            before_loop = count[0]
            with dve.Fori(1, ITERS - 1) as i:
                count[0] = 0
                where[0] = DVE_LINKS * i + (before_loop - DVE_LINKS)
                for job, off in EW_ORDER.body:
                    handle(job, i + off, 1 + off)
                assert count[0] == DVE_LINKS, count[0]
            where[0], count[0] = before_loop, (ITERS - 2) * DVE_LINKS
            for job, g in EW_ORDER.of(ITERS - 1):
                handle(job, g, g)

        @block.tensor
        def _(pe):
            mm = pe.matmul

            def exact3(o, l, r, start, stop):
                mm(o, l[HI], r[HI], start=start, stop=False)
                mm(o, l[HI], r[LO], start=False, stop=False)
                return mm(o, l[LO], r[HI], start=False, stop=stop)

            def handle(job, i, like):
                kind = job if isinstance(job, int) else job.rstrip("0123")
                last = {}
                for before, g in HELD_BY[job, like]:
                    name, per, n = READ_OUT[before]
                    last[name] = per, max(per * g + n, last[name][1] if name in last else 0)
                for name, (per, n) in last.items():
                    pe.wait_ge(S[name], per * (i - like) + n if per else n)
                if job == "U0" and like == 0:
                    pe.wait_ge(S["ones_r"], 2)
                    for _ in range(WARM_START):
                        mm(bank(job, like, 0)[:, 0:128], ones_r, ones_r, start=True, stop=True)
                for _ in range(WARM.get((job, like), 0)):
                    mm(bank(job, like, 0), sel_g[:, 0, 0:128], adj_s[:, HI, 0, :], start=True, stop=True)
                if kind == "W":
                    pe.wait_ge(S["ones_r"], 2)
                    for c in range(NC):
                        for hl in (HI, LO):
                            mm(bank(job, like, 0), ones_r, adj_s[:, hl, c, :],
                               start=(c == 0 and hl == HI), stop=(c == NC - 1 and hl == LO))
                    pe.wait_ge(S["ld_b"], 96)
                    mm(bank(job, like, 1)[:, 0:D], ones1, b1_t[0:1, :], start=True, stop=True)\
                        .then_inc(S["row_sums"], 1)
                elif kind == "P":
                    pe.wait_ge(S["keyed"], 1)
                    mm(bank(job, like, 0)[:, 0:E], C(C_ONES, C_ONES + 128)[0:1, :], tmp[0:1, 0:E],
                       start=True, stop=True).then_inc(S["keys_spread"], 1)
                elif kind == "E":
                    pe.wait_ge(S["ranked"], 1)
                    for k in range(2):
                        for c in range(EC):
                            mm(bank(job, like, 0)[:, k * E:(k + 1) * E], spread[:, 2 * k + c, :], perm[:, c, :],
                               start=(c == 0), stop=(c == EC - 1))
                    for rc in range(EC):
                        for c in range(EC):
                            m = mm(bank(job, like, 1)[:, rc:rc + 1], perm[:, c, rc * 128:(rc + 1) * 128],
                                   edge_f[:, c:c + 1], start=(c == 0), stop=(c == EC - 1))
                    m.then_inc(S["sorted"], 1)
                elif kind == "L":
                    pe.wait_ge(S["selections"], 1)
                    for ec in range(EC):
                        for c in range(NC):
                            for hl in (HI, LO):
                                m = mm(bank(job, like, ec), sel_g[:, c, E + ec * 128:E + (ec + 1) * 128],
                                       adj_s[:, hl, c, :], start=(c == 0 and hl == HI), stop=(c == NC - 1 and hl == LO))
                        m.then_inc(S["dst_rows"], 1)
                elif kind == "LN":
                    pe.wait_ge(S["ld_ident"], 32)
                    pe.wait_ge(S["edge_adj"], 1)
                    for ec in range(EC):
                        m = mm(bank(job, like, 0)[0:16, ec * 128:(ec + 1) * 128], spread_adj[:, ec, 0:16],
                               ident[:, :], start=True, stop=True)
                    m.then_inc(S["edge_rows"], 1)
                elif kind in ("U", "H"):
                    src, ready, full = (buf_a, "x_ready", "u_full") if kind == "U" else (buf_b, "z2_ready", "h2_full")
                    b = int(job[-1])
                    pe.wait_ge(S[ready], 4 * i + b + 1)
                    for c in range(NC):
                        if (job, like, b) == ("U0", 0, 0):
                            pe.wait_ge(S["adj_split"], c + 1)
                        m = exact3(bank(job, like, 0), [src[:, hl, b, c * 128:(c + 1) * 128] for hl in (HI, LO)],
                                   [adj_s[:, hl, c, :] for hl in (HI, LO)], c == 0, c == NC - 1)
                    m.then_inc(S[full], 1)
                elif kind == "Z":
                    if like == 0:
                        pe.wait_ge(S["w_split"], 1)
                    for b in PAIR[job]:
                        pe.wait_ge(S["u_ready"], 4 * i + b + 1)
                        exact3(bank(job, like, b % 2), [wg_s[:, hl, 0, :] for hl in (HI, LO)],
                               [buf_b[:, hl, b, :] for hl in (HI, LO)], True, True).then_inc(S["z_full"], 1)
                elif kind == "Y":
                    for b in PAIR[job]:
                        pe.wait_ge(S["h1_ready"], 4 * i + b + 1)
                        for c in range(NC):
                            m = exact3(bank(job, like, b % 2)[:, c * 128:(c + 1) * 128],
                                       [buf_a[:, hl, b, c * 128:(c + 1) * 128] for hl in (HI, LO)],
                                       [wg_s[:, hl, 1, :] for hl in (HI, LO)], True, True)
                        m.then_inc(S["z2_full"], 1)
                elif isinstance(job, int):
                    p, t, k, s = LSTM[job]
                    if job == 0:
                        if like == 0:
                            pe.wait_ge(S["lw_split0"], 1)
                            pe.wait_ge(S["lw_split1"], 1)
                        pe.wait_ge(S["h2_ready"], 8 * i + 8)
                    wi, wh = ([[wl_s[:, hl, m, p - 1, g * D:(g + 1) * D] for hl in (HI, LO)] for g in range(4)]
                              for m in range(2))
                    todo = gates_of(LSTM[job])
                    o = {g: cols(gate_bank(job, like, g), LSTM[job]) for g in todo}
                    tok = [toks(hl, LSTM[job]) for hl in (HI, LO)]

                    def products(w, r, made, first, last):
                        if made is not None:
                            pe.wait_ge(S["h_hi"], made)
                        for g in todo[:AHEAD]:
                            mm(o[g], w[g][HI], r[HI], start=first, stop=False)
                            mm(o[g], w[g][LO], r[HI], start=False, stop=False)
                        if made is not None:
                            pe.wait_ge(S["h_ready"], made)
                        for n, g in enumerate(todo):
                            if n >= AHEAD:
                                mm(o[g], w[g][HI], r[HI], start=first, stop=False)
                                mm(o[g], w[g][LO], r[HI], start=False, stop=False)
                            m = mm(o[g], w[g][HI], r[LO], start=False, stop=last)
                            if last:
                                m.then_inc(S["gate_full"], 1)

                    if p == 1:
                        for g in todo:
                            exact3(o[g], wi[g], tok, True, True).then_inc(S["gate_full"], 1)
                    else:
                        products(wi, tok, NL * i + done_before(job) if t == 0 else None, True, t == 0)
                    if t:
                        products(wh, [cols(rec[:, s, hl, :], LSTM[job]) for hl in (HI, LO)],
                                 NL * i + last_user(job) + 1, False, True)
                elif kind == "N":
                    b = int(job[1])
                    pe.wait_ge(S[f"hn_ready{b // 2}"], 4 * i + 2 * (b % 2) + 2)
                    for c in range(NC):
                        cc = slice(c * 128, (c + 1) * 128)
                        m = pe.transpose(bank(job, like, 0)[:, cc], hn[:, b, cc], ident[:, :])
                    m.then_inc(S["n_full"], 1)
                elif kind == "GX":
                    b = int(job[-1])
                    pe.wait_ge(S["x1_ready"], 4 * i + b + 1)
                    for c in range(NC):
                        for hl in (HI, LO):
                            m = mm(bank(job, like, 0), buf_c[:, hl, b, c * 128:(c + 1) * 128], sel_g[:, c, :],
                                   start=(c == 0 and hl == HI), stop=(c == NC - 1 and hl == LO))
                    m.then_inc(S["gx_full"], 1)
                elif kind in ("Q", "V"):
                    n = int(kind == "V")
                    k = int(job[-1])
                    pe.wait_ge(S["gx_ready"], 4 * i + 2 * k + 2)
                    exact3(bank(job, like, 0).rearrange("p (b e) -> p b e", b=2),
                           [wa_s[:, hl, n, :] for hl in (HI, LO)],
                           [buf_d[:, hl, 2 * k:2 * k + 2, n * E:(n + 1) * E] for hl in (HI, LO)], True, True)\
                        .then_inc(S["v_full" if n else "q_full"], 1)
                elif kind == "SC":
                    pe.wait_ge(S["lrelu_ready"], 2 * i + 2)
                    for b in range(G):
                        m = mm(bank(job, like, 0)[0:16, 0:E], a_blk[:, b, :],
                               hn[:, b // 2, (b % 2) * E:(b % 2 + 1) * E], start=(b == 0), stop=(b == G - 1))
                    m.then_inc(S["sc_full"], 1)
                elif kind == "AB":
                    k = int(job[2])
                    pe.wait_ge(S["attn_ready"], i + 1)
                    for b in range(2):
                        m = mm(bank(job, like, 0)[:, b * E:(b + 1) * E], eall[:, 2 * k + b, :], sm[:, 0, :],
                               start=True, stop=True)
                    m.then_inc(S["ab_full"], 1)
                elif kind == "MW":
                    pe.wait_ge(S["m_split"], 2 * i + 2)
                    ec = int(job[-1])
                    for b in range(G):
                        c0 = (b % 2) * E + ec * 128
                        m = exact3(bank(job, like, 0)[:, b * D:(b + 1) * D],
                                   [buf_c[:, hl, b // 2, c0:c0 + 128] for hl in (HI, LO)],
                                   [wa_s[:, hl, 2, :] for hl in (HI, LO)], True, True)
                    m.then_inc(S["mw_full"], 1)
                elif kind == "O":
                    pe.wait_ge(S["mw_ready"], 2 * i + 2)
                    c = int(job[1])
                    for ec in range(EC):
                        for hl in (HI, LO):
                            m = mm(bank(job, like, 0), sel_s[:, ec, c * 128:(c + 1) * 128], buf_c[:, hl, 2 + ec, :],
                                   start=(ec == 0 and hl == HI), stop=(ec == EC - 1 and hl == LO))
                    m.then_inc(S["out_full"], 1)

            in_order(pe, PE_ORDER, handle)


def kernel(x, adj, L0_gnn_Wg0, L0_gnn_bg0, L0_gnn_Wg1, L0_gnn_bg1, L0_gnn_Wih, L0_gnn_Whh, L0_gnn_bih,
           L0_gnn_bhh, L1_gnn_W_lin, L1_gnn_W_val, L1_gnn_a, L1_gnn_W_out, L1_gnn_src, L1_gnn_dst):
    import numpy as np
    import concourse.bacc as bacc
    from concourse.bass_utils import run_bass_kernel_spmd

    order = np.concatenate([np.arange(r, T, R) for r in range(R)])
    place = np.argsort(order)

    consts = np.zeros((128, C_END), np.float32)
    consts[:, C_ID:C_ID + 128] = np.eye(128)
    d, col = np.arange(128)[:, None], np.arange(16)[None, :]
    for b in range(G):
        consts[:, C_MASK + 16 * b:C_MASK + 16 * b + 16] = col == HEADS * b + d // (D // HEADS)
        consts[0:16, C_EALL + 128 * b:C_EALL + 128 * b + 128] = (col == HEADS * b + d // (D // HEADS)).T
    consts[:, C_NODE:C_NODE + NC] = order.reshape(NC, 128).T
    consts[:, C_NROW:C_NROW + T] = order
    consts[:, C_IOTA:C_IOTA + E] = np.arange(E)
    consts[:, C_EDGE:C_EDGE + EC] = np.arange(E).reshape(EC, 128).T
    consts[:, C_ONES:C_ONES + 128] = 1.0

    X = np.asarray(x)[:, order, :].reshape(ITERS, G, NC, 128, D).transpose(0, 3, 1, 2, 4)
    A = np.asarray(adj)[order][:, order].T.reshape(NC, 128, T).transpose(1, 0, 2)
    src, dst = np.asarray(L1_gnn_src), np.asarray(L1_gnn_dst)
    cols = np.concatenate([src.reshape(EC, 128), dst.reshape(EC, 128)]).T
    rows = src[None, :]

    def stack(ws):
        return np.concatenate([np.asarray(w) for w in ws], axis=1)

    def gate_cols(w):
        return np.asarray(w).transpose(2, 0, 1)

    def bias(v):
        return np.asarray(v).reshape(SKIPS, 4, D).transpose(2, 0, 1)

    arrays = {
        "x": X, "adjT": A, "consts": consts, "edge_col": cols, "edge_row": rows,
        "w_gnn": stack([L0_gnn_Wg0, L0_gnn_Wg1, np.asarray(L1_gnn_W_lin).T, np.asarray(L1_gnn_W_val).T,
                        np.asarray(L1_gnn_W_out).T]),
        "b_gnn0": np.asarray(L0_gnn_bg0)[:, None], "b_gnn1": np.asarray(L0_gnn_bg1)[None, :],
        "w_ih": gate_cols(L0_gnn_Wih), "w_hh": gate_cols(L0_gnn_Whh),
        "b_ih": bias(L0_gnn_bih), "b_hh": bias(L0_gnn_bhh),
        "a_col": np.asarray(L1_gnn_a).reshape(D, 1),
    }
    arrays = {k: np.ascontiguousarray(v) for k, v in arrays.items()}
    nc = bacc.Bacc("TRN2", target_bir_lowering=False, num_devices=1)
    args = {k: nc.dram_tensor(k, v.shape, mybir.dt.from_np(v.dtype), kind="ExternalInput").ap()
            for k, v in arrays.items()}
    out = nc.dram_tensor("out", (ITERS, 128, NC, G, D), mybir.dt.float32, kind="ExternalOutput").ap()
    build(nc, out=out, **args)
    r = run_bass_kernel_spmd(nc, [arrays], core_ids=[0])
    y = r.results[0]["out"].transpose(0, 3, 2, 1, 4).reshape(B, T, D)
    return np.ascontiguousarray(y[:, place, :])
```
